# Optimizing a Trainium2 kernel written in Bass

```python
import numpy as np
import jax
import jax.numpy as jnp

def _softmax(x, axis=-1):
    return jax.nn.softmax(x, axis=axis)

def _gelu(x):
    return jax.nn.gelu(x, approximate=True)

def _silu(x):
    return jax.nn.silu(x)

def _sigmoid(x):
    return jax.nn.sigmoid(x)

def _layernorm(x, axis=-1, eps=1e-05):
    m = jnp.mean(x, axis=axis, keepdims=True)
    v = jnp.var(x, axis=axis, keepdims=True)
    return (x - m) / jnp.sqrt(v + eps)

def _scatter_add(tgt, idx, src, axis=0):
    return tgt.at[idx].add(src)

def _segment_sum(src, seg, n):
    return jax.ops.segment_sum(src, seg, n)
kernel_name = 'mk_seq_preln_d2_jaxref_r8_e4fa82'

def setup_inputs(seed: int=0):
    np.random.seed(seed)
    _w = jnp.asarray

    def _L0_attn_setup():
        import jax, jax.numpy as jnp
        import numpy as np
        DIM = 256
        STATE = 64
        DT_RANK = 128
        CHUNK = 64
        key = jax.random.key(seed)
        ks = jax.random.split(key, 8)
        B, L, D, N, R = (4, 256, DIM, STATE, DT_RANK)
        x = jax.random.normal(ks[0], (B, L, D), dtype=jnp.float32)
        norm_w = jnp.ones((D,), jnp.float32)
        norm_b = jnp.zeros((D,), jnp.float32)
        x_proj_w = jax.random.normal(ks[1], (R + 2 * N, D), jnp.float32) * (1.0 / np.sqrt(D))
        dt_proj_w = jax.random.normal(ks[2], (D, R), jnp.float32) * (1.0 / np.sqrt(R))
        dt_proj_b = jax.random.normal(ks[3], (D,), jnp.float32) * 0.01
        A_log = jnp.log(jnp.tile(jnp.arange(1, N + 1, dtype=jnp.float32)[None, :], (D, 1)))
        D_param = jnp.ones((D,), jnp.float32)
        out_proj_w = jax.random.normal(ks[4], (D, D), jnp.float32) * (1.0 / np.sqrt(D))
        return {'x': x, 'norm_w': norm_w, 'norm_b': norm_b, 'x_proj_w': x_proj_w, 'dt_proj_w': dt_proj_w, 'dt_proj_b': dt_proj_b, 'A_log': A_log, 'D_param': D_param, 'out_proj_w': out_proj_w}
    _L0_attn_in = _L0_attn_setup()

    def _L0_ffn_setup():
        import jax, jax.numpy as jnp
        import numpy as np
        import math
        D_MODEL = 256
        D_FF = 1024
        NUM_EXPERTS = 8
        TOP_K = 2
        CAPACITY_FACTOR = 1.25
        BATCH, SEQ = (4, 256)

        def _moe_forward(x, Wg, w1, w2):
            B, T, d = x.shape
            S = B * T
            E, K = (NUM_EXPERTS, TOP_K)
            C = math.ceil(CAPACITY_FACTOR * S * K / E)
            xr = x.reshape(S, d)
            probs = jax.nn.softmax(xr @ Wg, axis=-1)
            gate_vals, expert_idx = jax.lax.top_k(probs, K)
            flat_e = expert_idx.reshape(-1)
            oh = jax.nn.one_hot(flat_e, E, dtype=jnp.int32)
            pos = jnp.sum((jnp.cumsum(oh, axis=0) - 1) * oh, axis=1)
            kept = pos < C
            i = jnp.arange(S * K)
            slot = i % K * S + i // K
            sentinel = S * K
            pos_w = jnp.where(kept, pos, C)
            dispatch_mask = jnp.full((E, C), sentinel, dtype=jnp.int32)
            dispatch_mask = dispatch_mask.at[flat_e, pos_w].set(slot.astype(jnp.int32), mode='drop')
            combine_weights = (gate_vals * kept.reshape(S, K)).T
            dispatched = xr[dispatch_mask.reshape(-1) % S].reshape(E, C, d)
            h = jax.nn.relu(jnp.einsum('ecd,edf->ecf', dispatched, w1))
            expert_out = jnp.einsum('ecf,efd->ecd', h, w2)
            rerouted = jnp.zeros((S * K + 1, d), dtype=expert_out.dtype)
            rerouted = rerouted.at[dispatch_mask.reshape(-1)].set(expert_out.reshape(-1, d))
            rerouted = rerouted[:-1].reshape(K, S, d)
            out = jnp.einsum('ks,ksm->sm', combine_weights, rerouted)
            return out.reshape(B, T, d)
        key = jax.random.key(seed)
        k1, k2, k3, k4 = jax.random.split(key, 4)
        x = jax.random.normal(k1, (BATCH, SEQ, D_MODEL), dtype=jnp.float32)
        Wg = jax.random.normal(k2, (D_MODEL, NUM_EXPERTS), dtype=jnp.float32) * 0.02
        w1 = jax.random.normal(k3, (NUM_EXPERTS, D_MODEL, D_FF), dtype=jnp.float32) * 0.02
        w2 = jax.random.normal(k4, (NUM_EXPERTS, D_FF, D_MODEL), dtype=jnp.float32) * 0.02
        return {'x': x, 'Wg': Wg, 'w1': w1, 'w2': w2}
    _L0_ffn_in = _L0_ffn_setup()

    def _L1_attn_setup():
        import jax, jax.numpy as jnp
        import numpy as np
        D_MODEL = 256
        N_HEADS = 16
        D_K = D_MODEL // N_HEADS
        EPS = 1e-06
        key = jax.random.key(seed)
        ks = jax.random.split(key, 9)
        s = 1.0 / np.sqrt(D_MODEL)
        return {'x': jax.random.normal(ks[0], (4, 512, D_MODEL), dtype=jnp.float32), 'Wq': jax.random.normal(ks[1], (D_MODEL, D_MODEL), dtype=jnp.float32) * s, 'bq': jnp.zeros((D_MODEL,), dtype=jnp.float32), 'Wk': jax.random.normal(ks[2], (D_MODEL, D_MODEL), dtype=jnp.float32) * s, 'bk': jnp.zeros((D_MODEL,), dtype=jnp.float32), 'Wv': jax.random.normal(ks[3], (D_MODEL, D_MODEL), dtype=jnp.float32) * s, 'bv': jnp.zeros((D_MODEL,), dtype=jnp.float32), 'Wo': jax.random.normal(ks[4], (D_MODEL, D_MODEL), dtype=jnp.float32) * s, 'bo': jnp.zeros((D_MODEL,), dtype=jnp.float32)}
    _L1_attn_in = _L1_attn_setup()

    def _L1_ffn_setup():
        import jax, jax.numpy as jnp
        import numpy as np
        DIM_IN = 256
        DIM_HIDDEN = 1024
        key = jax.random.key(seed)
        k_x, k_g, k_u, k_d = jax.random.split(key, 4)
        s_in = 1.0 / np.sqrt(DIM_IN)
        s_hid = 1.0 / np.sqrt(DIM_HIDDEN)
        x = jax.random.normal(k_x, (4, 256, DIM_IN), dtype=jnp.float32)
        w_gate = jax.random.uniform(k_g, (DIM_HIDDEN, DIM_IN), jnp.float32, -s_in, s_in)
        w_up = jax.random.uniform(k_u, (DIM_HIDDEN, DIM_IN), jnp.float32, -s_in, s_in)
        w_down = jax.random.uniform(k_d, (DIM_IN, DIM_HIDDEN), jnp.float32, -s_hid, s_hid)
        return {'x': x, 'w_gate': w_gate, 'w_up': w_up, 'w_down': w_down}
    _L1_ffn_in = _L1_ffn_setup()
    _d = {'L0_attn_x': _L0_attn_in['x'], 'L0_attn_norm_w': _L0_attn_in['norm_w'], 'L0_attn_norm_b': _L0_attn_in['norm_b'], 'L0_attn_x_proj_w': _L0_attn_in['x_proj_w'], 'L0_attn_dt_proj_w': _L0_attn_in['dt_proj_w'], 'L0_attn_dt_proj_b': _L0_attn_in['dt_proj_b'], 'L0_attn_A_log': _L0_attn_in['A_log'], 'L0_attn_D_param': _L0_attn_in['D_param'], 'L0_attn_out_proj_w': _L0_attn_in['out_proj_w'], 'L0_ffn_Wg': _L0_ffn_in['Wg'], 'L0_ffn_w1': _L0_ffn_in['w1'], 'L0_ffn_w2': _L0_ffn_in['w2'], 'L1_attn_Wq': _L1_attn_in['Wq'], 'L1_attn_bq': _L1_attn_in['bq'], 'L1_attn_Wk': _L1_attn_in['Wk'], 'L1_attn_bk': _L1_attn_in['bk'], 'L1_attn_Wv': _L1_attn_in['Wv'], 'L1_attn_bv': _L1_attn_in['bv'], 'L1_attn_Wo': _L1_attn_in['Wo'], 'L1_attn_bo': _L1_attn_in['bo'], 'L1_ffn_w_gate': _L1_ffn_in['w_gate'], 'L1_ffn_w_up': _L1_ffn_in['w_up'], 'L1_ffn_w_down': _L1_ffn_in['w_down']}
    _x0 = _d['L0_attn_x']
    _d['L0_attn_x'] = jax.random.normal(jax.random.fold_in(jax.random.key(seed), 1), (2, 1024, 256), dtype=_x0.dtype)
    del _x0
    return _d

def reference(L0_attn_x, L0_attn_norm_w, L0_attn_norm_b, L0_attn_x_proj_w, L0_attn_dt_proj_w, L0_attn_dt_proj_b, L0_attn_A_log, L0_attn_D_param, L0_attn_out_proj_w, L0_ffn_Wg, L0_ffn_w1, L0_ffn_w2, L1_attn_Wq, L1_attn_bq, L1_attn_Wk, L1_attn_bk, L1_attn_Wv, L1_attn_bv, L1_attn_Wo, L1_attn_bo, L1_ffn_w_gate, L1_ffn_w_up, L1_ffn_w_down):

    def _L0_attn_ref(x, norm_w, norm_b, x_proj_w, dt_proj_w, dt_proj_b, A_log, D_param, out_proj_w):
        import jax, jax.numpy as jnp
        import numpy as np
        DIM = 256
        STATE = 64
        DT_RANK = 128
        CHUNK = 64
        B, L, D = x.shape
        N = STATE
        mu = jnp.mean(x, axis=-1, keepdims=True)
        var = jnp.var(x, axis=-1, keepdims=True)
        xn = (x - mu) / jnp.sqrt(var + 1e-05) * norm_w + norm_b
        proj = xn @ x_proj_w.T
        R = dt_proj_w.shape[1]
        delta, B_ssm, C_ssm = jnp.split(proj, [R, R + N], axis=-1)
        delta = jax.nn.softplus(delta @ dt_proj_w.T + dt_proj_b)
        A = -jnp.exp(A_log)
        c_idx = jnp.arange(L) % CHUNK
        C_used = C_ssm[:, c_idx, :]

        def step(h, inp):
            dt, b, xt, c = inp
            dA = jnp.exp(dt[:, :, None] * A)
            h = dA * h + dt[:, :, None] * b[:, None, :] * xt[:, :, None]
            y = jnp.einsum('bdn,bn->bd', h, c)
            return (h, y)
        h0 = jnp.zeros((B, D, N), x.dtype)
        xs = (jnp.moveaxis(delta, 1, 0), jnp.moveaxis(B_ssm, 1, 0), jnp.moveaxis(xn, 1, 0), jnp.moveaxis(C_used, 1, 0))
        _, ys = jax.lax.scan(step, h0, xs)
        y = jnp.moveaxis(ys, 0, 1)
        return (y + x * D_param) @ out_proj_w.T

    def _L0_ffn_ref(x, Wg, w1, w2):
        import jax, jax.numpy as jnp
        import numpy as np
        import math
        D_MODEL = 256
        D_FF = 1024
        NUM_EXPERTS = 8
        TOP_K = 2
        CAPACITY_FACTOR = 1.25
        BATCH, SEQ = (4, 256)

        def _moe_forward(x, Wg, w1, w2):
            B, T, d = x.shape
            S = B * T
            E, K = (NUM_EXPERTS, TOP_K)
            C = math.ceil(CAPACITY_FACTOR * S * K / E)
            xr = x.reshape(S, d)
            probs = jax.nn.softmax(xr @ Wg, axis=-1)
            gate_vals, expert_idx = jax.lax.top_k(probs, K)
            flat_e = expert_idx.reshape(-1)
            oh = jax.nn.one_hot(flat_e, E, dtype=jnp.int32)
            pos = jnp.sum((jnp.cumsum(oh, axis=0) - 1) * oh, axis=1)
            kept = pos < C
            i = jnp.arange(S * K)
            slot = i % K * S + i // K
            sentinel = S * K
            pos_w = jnp.where(kept, pos, C)
            dispatch_mask = jnp.full((E, C), sentinel, dtype=jnp.int32)
            dispatch_mask = dispatch_mask.at[flat_e, pos_w].set(slot.astype(jnp.int32), mode='drop')
            combine_weights = (gate_vals * kept.reshape(S, K)).T
            dispatched = xr[dispatch_mask.reshape(-1) % S].reshape(E, C, d)
            h = jax.nn.relu(jnp.einsum('ecd,edf->ecf', dispatched, w1))
            expert_out = jnp.einsum('ecf,efd->ecd', h, w2)
            rerouted = jnp.zeros((S * K + 1, d), dtype=expert_out.dtype)
            rerouted = rerouted.at[dispatch_mask.reshape(-1)].set(expert_out.reshape(-1, d))
            rerouted = rerouted[:-1].reshape(K, S, d)
            out = jnp.einsum('ks,ksm->sm', combine_weights, rerouted)
            return out.reshape(B, T, d)
        return _moe_forward(x, Wg, w1, w2)

    def _L1_attn_ref(x, Wq, bq, Wk, bk, Wv, bv, Wo, bo):
        import jax, jax.numpy as jnp
        import numpy as np
        D_MODEL = 256
        N_HEADS = 16
        D_K = D_MODEL // N_HEADS
        EPS = 1e-06
        b, n, _ = x.shape
        h, d = (N_HEADS, D_K)

        def proj(W, bias):
            y = jnp.einsum('bnm,dm->bnd', x, W) + bias
            return y.reshape(b, n, h, d).transpose(0, 2, 1, 3)
        Q = jax.nn.relu(proj(Wq, bq))
        K = jax.nn.relu(proj(Wk, bk))
        V = proj(Wv, bv)
        pos = jnp.arange(n, dtype=x.dtype)
        decay = jnp.exp(-pos / n)[None, None, :, None]
        Q = Q * decay
        K = K * decay
        KV = jnp.einsum('bhnd,bhne->bhde', K, V)
        Ksum = K.sum(axis=2)
        Z = 1.0 / (jnp.einsum('bhnd,bhd->bhn', Q, Ksum)[..., None] + EPS)
        out = jnp.einsum('bhnd,bhde->bhne', Q, KV) * Z
        out = out.transpose(0, 2, 1, 3).reshape(b, n, h * d)
        return jnp.einsum('bnm,dm->bnd', out, Wo) + bo

    def _L1_ffn_ref(x, w_gate, w_up, w_down):
        import jax, jax.numpy as jnp
        import numpy as np
        DIM_IN = 256
        DIM_HIDDEN = 1024
        gate = jnp.einsum('bsd,hd->bsh', x, w_gate)
        up = jnp.einsum('bsd,hd->bsh', x, w_up)
        gated = jax.nn.silu(gate) * up
        return jnp.einsum('bsh,dh->bsd', gated, w_down)
    x = L0_attn_x
    x = x + _L0_attn_ref(_layernorm(x, axis=-1), L0_attn_norm_w, L0_attn_norm_b, L0_attn_x_proj_w, L0_attn_dt_proj_w, L0_attn_dt_proj_b, L0_attn_A_log, L0_attn_D_param, L0_attn_out_proj_w)
    x = x + _L0_ffn_ref(_layernorm(x, axis=-1), L0_ffn_Wg, L0_ffn_w1, L0_ffn_w2)
    x = x + _L1_attn_ref(_layernorm(x, axis=-1), L1_attn_Wq, L1_attn_bq, L1_attn_Wk, L1_attn_bk, L1_attn_Wv, L1_attn_bv, L1_attn_Wo, L1_attn_bo)
    x = x + _L1_ffn_ref(_layernorm(x, axis=-1), L1_ffn_w_gate, L1_ffn_w_up, L1_ffn_w_down)
    return x

_drawn_inputs = setup_inputs


def setup_inputs(seed=0):
    import zlib

    import numpy as np

    out = dict(_drawn_inputs(seed))
    spreads = {'L0_attn_norm_w': (1.0, 0.2),
     'L0_attn_norm_b': (0.0, 0.1),
     'L0_attn_D_param': (1.0, 0.6),
     'L1_attn_bq': (0.0, 2.0),
     'L1_attn_bk': (0.0, 2.0),
     'L1_attn_bv': (0.0, 0.789),
     'L1_attn_bo': (0.0, 0.8)}
    factors = {'L0_attn_dt_proj_b': 8.0,
     'L0_ffn_Wg': 8.0,
     'L0_ffn_w1': 8.0,
     'L0_ffn_w2': 8.0,
     'L1_attn_Wq': 8.0,
     'L1_attn_Wk': 8.0,
     'L1_attn_Wv': 8.0,
     'L1_attn_Wo': 4.392,
     'L1_ffn_w_gate': 5.389,
     'L1_ffn_w_up': 5.174,
     'L1_ffn_w_down': 5.188}
    for name, (base, spread) in spreads.items():
        noise = np.random.default_rng([zlib.crc32(name.encode()), seed]).standard_normal(out[name].shape)
        drawn = base * np.exp(spread * noise) if base else spread * noise
        out[name] = jnp.asarray(drawn.astype(out[name].dtype))
    for name, factor in factors.items():
        out[name] = (out[name] * factor).astype(out[name].dtype)
    return out
```

```python
from contextlib import ExitStack

import numpy as np
import concourse.bass as bass
from concourse import mybir

P = 128
F32 = mybir.dt.float32
BF16 = mybir.dt.bfloat16
U32 = mybir.dt.uint32
ALU = mybir.AluOpType
ACT = mybir.ActivationFunctionType
AX = mybir.AxisListType

BATCH, SEQ, D = 2, 1024, 256
TOK = BATCH * SEQ
TILES = TOK // P
DH = D // P
RANK, STATE, CSPAN = 128, 64, 64
EXPERTS, FF = 8, 1024
CAP = -(-5 * TOK * 2 // (4 * EXPERTS))
SLOTS = EXPERTS * CAP
ST = CAP // P
FT = FF // P
HEADS, DK = 16, 16
EPS = 1e-5

T = 128
CHUNKS = TOK // T
CPB = SEQ // T
G = 8
GROUPS = P // G
ROWG = 4
RCH = P // ROWG
LAG = 2
ON_POOL = (1, 4, 7, 9, 12, 15)
W = T + 1


class Mark:

    def __init__(self, sem, value):
        self.sem, self.value = sem, value


class Count:

    def __init__(self, sem):
        self.sem, self.n = sem, 0

    def up(self, ins, by):
        self.n += by
        ins.then_inc(self.sem, by)
        return Mark(self.sem, self.n)

    def dma(self, ins):
        return self.up(ins, 16)

    def all(self):
        return Mark(self.sem, self.n)


class Engine:

    def __init__(self, queue, sem):
        self.q, self.count, self.met = queue, Count(sem), {}

    def mark(self, ins):
        return self.count.up(ins, 1)

    def wait(self, *marks):
        for m in marks:
            if m is not None and m.value > self.met.get(id(m.sem), 0):
                self.q.wait_ge(m.sem, m.value)
                self.met[id(m.sem)] = m.value


class Program:
    def __init__(self, nc, ctx):
        self.nc, self.ctx = nc, ctx
        self.pe = Engine(nc.tensor, self.sem("pe"))
        self.act = Engine(nc.scalar, self.sem("act"))
        self.dve = Engine(nc.vector, self.sem("dve"))
        self.pool = Engine(nc.gpsimd, self.sem("pool"))
        self.sp = Engine(nc.sync, self.sem("sp"))
        self.psum = ctx.enter_context(nc.psum_tensor("psum", [P, 8 * 512], F32))
        self.banks = [self.psum[:, 512 * i:512 * (i + 1)] for i in range(8)]

    def sem(self, name):
        return self.ctx.enter_context(self.nc.semaphore("s_" + name))

    def count(self, name):
        return Count(self.sem(name))

    def sb(self, name, shape, dt=F32, ctx=None):
        return (ctx or self.ctx).enter_context(self.nc.sbuf_tensor(name, shape, dt))

    def dram(self, name, shape, dt=F32):
        return self.nc.dram_tensor(name, shape, dt).ap()

    def ring(self, n, first=0):
        return Banks(self, list(range(first, first + n)))


class Banks:
    def __init__(self, p, which):
        self.p, self.which, self.at, self.free = p, which, 0, {}

    def take(self):
        b = self.which[self.at % len(self.which)]
        self.at += 1
        self.p.pe.wait(*self.free.get(b, ()))
        return b, self.p.banks[b]

    def read_by(self, b, *marks):
        self.free[b] = marks


def layer_norm_stats(p, src, tiles, stats, mom, sd, rstd, eps, src_ready):
    dve, act = p.dve, p.act
    for i in tiles:
        dve.wait(src_ready[i])
        m = dve.mark(dve.q.bn_stats(stats[:, i, :], src[:, i, :]))
    dve.wait(m)
    for i in tiles:
        m = dve.mark(dve.q.bn_aggr(mom[:, i, :], stats[:, i, :]))
    a, b = tiles[0], tiles[-1] + 1
    act.wait(m)
    m = act.mark(act.q.activation(sd[:, a:b], mom[:, a:b, 1], ACT.Sqrt, bias=eps[:, 0:1]))
    dve.wait(m)
    m = dve.mark(dve.q.reciprocal(rstd[:, a:b], sd[:, a:b]))
    dve.wait(m)


def normalize(p, dst, src, tiles, mom, rstd):
    dve = p.dve
    return {i: dve.mark(dve.q.tensor_scalar(dst[:, i, :], src[:, i, :], mom[:, i, 0:1], rstd[:, i:i + 1],
                                            ALU.subtract, ALU.mult)) for i in tiles}


def transpose_block(p, ring, src, ready, tiles, dh, ident):
    pe = p.pe
    b, bank = ring.take()
    for n, i in enumerate(tiles):
        pe.wait(ready[i])
        ins = pe.q.transpose(bank[:, n * P:(n + 1) * P], src[:, i, dh * P:(dh + 1) * P], ident[:, :])
    return b, bank, pe.mark(ins)


def build(nc, a, out):
    with ExitStack() as ctx:
        p = Program(nc, ctx)
        pe, act, dve, pool, sp = p.pe, p.act, p.dve, p.pool, p.sp

        parts_d = p.dram("parts_d", [CHUNKS, 6, DH, P, T], BF16)
        decay_parts_d = p.dram("decay_parts_d", [3, DH, P, STATE], BF16)
        skip_d = p.dram("skip_d", [P, DH, TOK])
        x1_d = p.dram("x1_d", [TOK, D])
        disp_d = p.dram("disp_d", [SLOTS + 1, D])
        eout_d = p.dram("eout_d", [SLOTS + 1, D])

        ident = p.sb("ident", [P, P])
        cols = p.sb("cols", [P, 7, DH])
        eps = p.sb("eps", [P, 1])
        gates = p.sb("gates", [P, 2, TILES])
        slots = p.sb("slots", [P, 2, TILES], U32)
        one = p.sb("one", [P, 1])
        consts = p.count("consts")
        consts.dma(sp.q.dma_start(ident[:, :], a["c_ident"]))
        m_const = consts.dma(sp.q.dma_start(cols[:, :, :], a["cols"]))
        norm_w, norm_b, skip_w, dt_b, bq, a_pad, b_pad = (cols[:, i, :] for i in range(7))
        pool.q.memset(eps[:, :], EPS)
        m_eps = pool.mark(pool.q.memset(one[:, :], 1.0))

        with ExitStack() as scan_ctx:
            sb = lambda name, shape, dt=F32: p.sb(name, shape, dt, scan_ctx)
            bmat = sb("bmat", [P, TOK])
            cmat = sb("cmat", [P, BATCH, CSPAN])
            cstat = sb("cstat", [P, CSPAN, 32])
            astat = sb("astat", [P, P, P], BF16)
            sel = sb("sel", [P, ROWG, P], BF16)
            prepare(p, a, dict(ident=ident, norm_w=norm_w, norm_b=norm_b, skip_w=skip_w, dt_b=dt_b, eps=eps,
                               one=one, bmat=bmat, cmat=cmat, cstat=cstat, astat=astat, sel=sel, m_const=m_const, m_eps=m_eps,
                               parts_d=parts_d, decay_parts_d=decay_parts_d, skip_d=skip_d, disp_d=disp_d,
                               eout_d=eout_d))
            nc.all_engine_barrier()
            selective_scan(p, a, dict(ident=ident, bmat=bmat, cstat=cstat, astat=astat, sel=sel,
                                      parts_d=parts_d, skip_d=skip_d, x1_d=x1_d, cmat=cmat, eps=eps,
                                      disp_d=disp_d, gates=gates, slots=slots))
            nc.all_engine_barrier()
        rest(p, a, out, dict(gates=gates, slots=slots, ident=ident, bq=bq, eps=eps, one=one, x1_d=x1_d, disp_d=disp_d, eout_d=eout_d))


def split3(p, v, hi, mid, lo, rest, free):
    act, dve = p.act, p.dve
    m = act.mark(act.q.copy(hi, v))
    dve.wait(m, *free)
    m = dve.mark(dve.q.tensor_tensor(rest, v, hi, ALU.subtract))
    act.wait(m)
    m = act.mark(act.q.copy(mid, rest))
    dve.wait(m)
    return dve.mark(dve.q.tensor_tensor(lo, rest, mid, ALU.subtract))


def prepare(p, a, s):
    pe, act, dve, pool, sp = p.pe, p.act, p.dve, p.pool, p.sp
    ident = s["ident"]
    with ExitStack() as ctx:
        sb = lambda name, shape, dt=F32: p.sb(name, shape, dt, ctx)
        xa = sb("xa", [P, TILES, D])
        x1 = sb("x1n", [P, TILES, D])
        xn_t = sb("xn_t", [P, DH, TOK])
        skip = sb("skip", [P, DH, TOK])
        w_proj = sb("w_proj", [P, DH, 3, P])
        w_dt = sb("w_dt", [P, D])
        delta = sb("delta", [P, 2, 512])
        sp_e = sb("sp_e", [P, DH, TOK])
        sp_r = sb("sp_r", [P, DH, TOK])
        parts = sb("parts", [P, 2, 6, DH, 512], BF16)
        rest = sb("rest", [P, 2, DH, 512])
        stats = sb("stats", [P, TILES, 6])
        mom = sb("mom", [P, TILES, 2])
        sd = sb("sd", [P, TILES])
        rstd = sb("rstd", [P, TILES])
        zero = sb("zero", [P, 2048])
        a_sb = sb("a_sb", [P, DH, STATE])
        sel_f = sb("sel_f", [P, ROWG, P])
        a_rest = sb("a_rest", [P, DH, STATE])
        a_parts = sb("a_parts", [P, 3, DH, STATE], BF16)

        x_in = a["x"].rearrange("b (i p) d -> p (b i) d", p=P)
        x_ready = {}
        for blk in range(4):
            c = p.count(f"x{blk}")
            m = c.dma(sp.q.dma_start(xa[:, 4 * blk:4 * blk + 4, :], x_in[:, 4 * blk:4 * blk + 4, :]))
            x_ready.update({i: m for i in range(4 * blk, 4 * blk + 4)})
        weights = p.count("w0")
        weights.dma(act.q.dma_start(w_proj[:, :, :, :], a["w_proj"]))
        weights.dma(act.q.dma_start(w_dt[:, :], a["w_dt"]))
        m_w = weights.dma(act.q.dma_start(a_sb[:, :, :], a["a_log"]))
        selc = p.count("selc")
        m_sel = selc.dma(act.q.dma_start(sel_f[:, :, :], a["c_sel"]))

        m_zero = pool.mark(pool.q.memset(zero[:, :], 0.0))
        pool.q.memset(s["cstat"][:, :, :], 0.0)
        m_a0 = pool.mark(pool.q.memset(s["astat"][:, :, :].bitcast(F32), 0.0))
        pool.wait(m_sel)
        pool.q.tensor_copy(s["sel"][:, :, :], sel_f[:, :, :])
        zeros = p.count("zeros")
        sp.wait(m_zero)
        for e in range(5):
            zeros.dma(sp.q.dma_start(s["disp_d"][e * 1024:(e + 1) * 1024, :].rearrange("(p r) d -> p (r d)", p=P),
                                     zero[:, :]))
        zeros.dma(sp.q.dma_start(s["eout_d"][SLOTS:SLOTS + 1, :], zero[0:1, 0:D]))

        act.wait(m_w)
        m = act.mark(act.q.activation(a_sb[:, :, :], a_sb[:, :, :], ACT.Exp))
        act.wait(m)
        m = act.mark(act.q.mul(a_sb[:, :, :], a_sb[:, :, :], -1.0))
        act.wait(m)
        m = split3(p, a_sb[:, :, :], a_parts[:, 0, :, :], a_parts[:, 1, :, :], a_parts[:, 2, :, :],
                   a_rest[:, :, :], [m])
        aw = p.count("aw")
        pool.wait(m)
        for k in range(3):
            m = aw.dma(pool.q.dma_start(s["decay_parts_d"][k].rearrange("h p n -> p h n"), a_parts[:, k, :, :]))
        pool.wait(m, m_a0)
        al = p.count("al")
        for g in range(ROWG):
            for dh in range(DH):
                for k, (first, n) in enumerate(((0, 3), (12, 2), (16, 1))):
                    row = 32 * g + first + dh
                    al.dma(pool.q.dma_start(
                        s["astat"][row:row + 2 * n - 1:2, RCH * g:RCH * (g + 1), dh * STATE:(dh + 1) * STATE],
                        s["decay_parts_d"][k:k + 1, dh, RCH * g:RCH * (g + 1), :].broadcast_to([n, RCH, STATE])))

        every = list(range(TILES))
        x1_ready, xh_ready = {}, {}
        act.wait(s["m_eps"])

        def norms(blk):
            tiles = every[4 * blk:4 * blk + 4]
            layer_norm_stats(p, xa, tiles, stats, mom, sd, rstd, s["eps"], x_ready)
            x1_ready.update(normalize(p, x1, xa, tiles, mom, rstd))
            layer_norm_stats(p, x1, tiles, stats, mom, sd, rstd, s["eps"], x1_ready)
            xh_ready.update(normalize(p, xa, x1, tiles, mom, rstd))

        ring = p.ring(8)
        pe.wait(s["m_const"], weights.all())
        act.wait(s["m_const"], s["m_eps"])
        dve.wait(s["m_const"])
        delta_free, parts_free, rest_free = {}, {}, {}
        zs, skip_m, stores = {}, {}, {}
        spill = p.count("spill")
        spill_parts = [p.count(f"spill_parts{i}") for i in range(2)]
        xn_ms, e_m, r_m = {}, {}, {}

        def project(blk):
            tiles = every[4 * blk:4 * blk + 4]
            t5 = slice(512 * blk, 512 * blk + 512)
            xn_m = xn_ms[blk] = []
            for dh in range(DH):
                b, bank, m = transpose_block(p, ring, xa, xh_ready, tiles, dh, ident)
                act.wait(m)
                m = act.mark(act.q.activation(xn_t[:, dh, t5], bank[:, :], ACT.Identity,
                                              bias=s["norm_b"][:, dh:dh + 1], scale=s["norm_w"][:, dh:dh + 1]))
                ring.read_by(b, m)
                xn_m.append(m)
                b, bank, m = transpose_block(p, ring, x1, x1_ready, tiles, dh, ident)
                dve.wait(m)
                m = dve.mark(dve.q.tensor_scalar(skip[:, dh, t5], bank[:, :], s["skip_w"][:, dh:dh + 1], None,
                                                 ALU.mult))
                ring.read_by(b, m)
                sp.wait(m)
                spill.dma(sp.q.dma_start(s["skip_d"][:, dh, t5], skip[:, dh, t5]))
            pe.wait(*xn_m)
            for j in range(2):
                b, bank = ring.take()
                for dh in range(DH):
                    ins = pe.q.matmul(bank[:, :], w_proj[:, dh, j, :], xn_t[:, dh, t5], start=dh == 0, stop=dh == 1)
                m = pe.mark(ins)
                act.wait(m, delta_free.get(blk % 2) if j == 0 else None)
                dst = delta[:, blk % 2, :] if j == 0 else s["bmat"][:, t5]
                m = act.mark(act.q.copy(dst, bank[:, :]))
                ring.read_by(b, m)
                if j == 0:
                    m_delta = m
            if blk % 2 == 0:
                b, bank = ring.take()
                for dh in range(DH):
                    ins = pe.q.matmul(bank[:, 0:CSPAN], w_proj[:, dh, 2, :], xn_t[:, dh, 512 * blk:512 * blk + CSPAN],
                                      start=dh == 0, stop=dh == 1)
                m = pe.mark(ins)
                act.wait(m)
                m = act.mark(act.q.copy(s["cmat"][:, blk // 2, :], bank[:, 0:CSPAN]))
                ring.read_by(b, m)
            pe.wait(m_delta)
            for dh in range(DH):
                b, bank = ring.take()
                m = pe.mark(pe.q.matmul(bank[:, :], w_dt[:, dh * P:(dh + 1) * P], delta[:, blk % 2, :],
                                        start=True, stop=True))
                act.wait(m)
                ma = act.mark(act.q.activation(sp_e[:, dh, t5], bank[:, :], ACT.Abs, bias=s["dt_b"][:, dh:dh + 1]))
                dve.wait(ma)
                mr = dve.mark(dve.q.tensor_scalar(sp_r[:, dh, t5], bank[:, :], s["dt_b"][:, dh:dh + 1], 0.0,
                                                  ALU.add, ALU.max))
                ring.read_by(b, ma, mr)
            delta_free[blk % 2] = m
            e_m[blk], r_m[blk] = ma, mr

        def split(blk):
            t5 = slice(512 * blk, 512 * blk + 512)
            act.wait(e_m[blk])
            m = act.mark(act.q.activation(sp_e[:, :, t5], sp_e[:, :, t5], ACT.Exp, scale=-1.0))
            act.wait(m)
            m = act.mark(act.q.activation(sp_e[:, :, t5], sp_e[:, :, t5], ACT.Ln, bias=s["one"][:, 0:1]))
            dve.wait(m, r_m[blk], *xn_ms[blk])
            m_dt = dve.mark(dve.q.tensor_tensor(sp_e[:, :, t5], sp_e[:, :, t5], sp_r[:, :, t5], ALU.add))
            dve.wait(m_dt)
            m_dtx = dve.mark(dve.q.tensor_tensor(sp_r[:, :, t5], sp_e[:, :, t5], xn_t[:, :, t5], ALU.mult))
            act.wait(m_dt, *stores.get(blk % 2, ()))
            dve.wait(*stores.get(blk % 2, ()))
            part = lambda n, k: parts[:, blk % 2, 3 * n + k, :, :]
            vs, m_v = (sp_e[:, :, t5], sp_r[:, :, t5]), (m_dt, m_dtx)
            m_hi, m_rest, m_mid, done = {}, {}, {}, []
            for n in range(2):
                act.wait(m_v[n])
                m_hi[n] = act.mark(act.q.copy(part(n, 0), vs[n]))
            for n in range(2):
                dve.wait(m_hi[n], rest_free.get(n))
                m_rest[n] = dve.mark(dve.q.tensor_tensor(rest[:, n, :, :], vs[n], part(n, 0), ALU.subtract))
            for n in range(2):
                act.wait(m_rest[n])
                m_mid[n] = act.mark(act.q.copy(part(n, 1), rest[:, n, :, :]))
            for n in range(2):
                dve.wait(m_mid[n])
                done.append(dve.mark(dve.q.tensor_tensor(part(n, 2), rest[:, n, :, :], part(n, 1), ALU.subtract)))
                rest_free[n] = done[-1]
            sp.wait(*done)
            for part in range(6):
                for dh in range(DH):
                    m = spill_parts[blk % 2].dma(sp.q.dma_start(
                        s["parts_d"][4 * blk:4 * blk + 4, part, dh].rearrange("c p t -> p c t"),
                        parts[:, blk % 2, part, dh, :].rearrange("p (c t) -> p c t", t=T)))
            stores[blk % 2] = (m,)

        for step, blk in ((norms, 0), (norms, 1), (project, 0), (norms, 2), (project, 1), (split, 0), (norms, 3),
                          (project, 2), (split, 1), (project, 3), (split, 2), (split, 3)):
            step(blk)
        sp.wait(spill.all(), spill_parts[0].all(), spill_parts[1].all(), zeros.all(), al.all())


def selective_scan(p, a, s):
    pe, act, dve, pool, sp = p.pe, p.act, p.dve, p.pool, p.sp
    NB = 3
    with ExitStack() as ctx:
        sb = lambda name, shape, dt=F32: p.sb(name, shape, dt, ctx)
        h = sb("h", [P, 3, P // 2, W])
        rows = sb("rows", [P, 2, RCH, T], BF16)
        decay = sb("decay", [P, NB, G, W])
        inp = sb("inp", [P, NB, G, W])
        w_out = sb("w_out", [P, DH, D])
        skip = sb("skip_c", [P, 2, DH, T])
        xres = sb("xres", [P, 2, D])
        y_sb = sb("y_sb", [P, 2, P])
        y_t = sb("y_t", [P, DH, T])
        x1o = sb("x1o", [P, Router.N, D])
        router = Router(p, a, ctx, s["gates"], s["slots"], s["ident"], s["eps"], s["disp_d"])
        z_used = [None]

        wo = p.count("wo0")
        wo.dma(act.q.dma_start(w_out[:, :, :], a["w_out"]))
        m_rows0 = pool.mark(pool.q.memset(rows[:, :, :, :].bitcast(F32), 0.0))
        m_decay0 = pool.mark(pool.q.memset(decay[:, :, :, 0:1], 0.0))
        rows_ld = [p.count(f"rows{i}") for i in range(2)]
        skip_ld = [p.count(f"skipld{i}") for i in range(2)]
        xres_ld = [p.count(f"xresld{i}") for i in range(2)]
        x1_st = [p.count(f"x1st{i}") for i in range(Router.N)]
        x_flat = a["x"].rearrange("b s d -> (b s) d")

        bank_a = [p.banks[0], p.banks[1]]
        bank_x = [p.psum[:, 1024:2048], p.psum[:, 2048:3072]]
        bank_y, bank_z = p.banks[6], p.banks[7]
        exp_m, prod_m, inp_m, ready_m, scan_m, carry_m = {}, {}, {}, {}, {}, {}
        rows_m, skip_m, xres_m, pe_done = {}, {}, {}, {}
        y_m, y_read, epi = {}, {}, {}
        store_m, resid_m, proj_m = {}, {}, {}

        def place_c(b):
            act.wait(y_m.get(CPB * b - 1))
            for dh in range(DH):
                r = slice(STATE * dh, STATE * (dh + 1))
                flat = s["cstat"][r, :, :].rearrange("p (q j) c -> p q (j c)", q=4)
                m = act.mark(act.q.copy(flat[:, :, dh:dh + 34 * 15 + 1:34],
                                        s["cmat"][r, b, :].rearrange("p (q j) -> p q j", q=4)))
            return m

        def half_slot(c, half):
            return c % 2 if half == 0 else 2

        def load(c):
            sp.wait(pe_done.get(c - 2), m_rows0)
            q = rows_ld[c % 2]
            for g in range(ROWG):
                src = s["parts_d"][c].rearrange("k h p t -> (k h) p t")[:, RCH * g:RCH * (g + 1), :]
                for first, n in ((0, 12), (12, 4), (16, 2)):
                    rows_m[c] = q.dma(sp.q.dma_start(rows[32 * g + first:32 * g + first + n, c % 2, :, :], src[0:n]))
            sp.wait(*(epi.get(c - 2, ())))
            skip_m[c] = skip_ld[c % 2].dma(sp.q.dma_start(skip[:, c % 2, :, :], s["skip_d"][:, :, c * T:(c + 1) * T]))
            xres_m[c] = xres_ld[c % 2].dma(sp.q.dma_start(xres[:, c % 2, :], x_flat[c * T:(c + 1) * T, :]))

        def stream(gi):
            c, k = divmod(gi, GROUPS)
            g = G * k // RCH
            pe.wait(rows_m[c])
            pe.wait(inp_m.get(gi - 2))
            for half in range(2):
                dp = G * k + 4 * half
                ins = pe.q.matmul(bank_x[gi % 2][:, 512 * half:512 * (half + 1)], s["sel"][:, g, :],
                                  rows[:, c % 2, dp % RCH:dp % RCH + 4, :], start=True, stop=True)
            bx = pe.mark(ins)
            for half in range(2):
                e = 2 * gi + half
                pe.wait(exp_m.get(e - 2))
                for j in range(4):
                    dp = G * k + 4 * half + j
                    ins = pe.q.matmul(bank_a[half][:, j * T:(j + 1) * T], s["astat"][:, dp, :],
                                      rows[:, c % 2, dp % RCH, :], start=True, stop=True)
                prod_m[e] = pe.mark(ins)
            if k == GROUPS - 1:
                pe_done[c] = prod_m[2 * gi + 1]
            pool.wait(scan_m.get(gi - NB))
            first = inp[:, gi % NB, :, 0:1]
            if c % CPB == 0:
                carry_m[gi] = pool.mark(pool.q.memset(first, 0.0))
            else:
                pool.wait(scan_m[gi - GROUPS])
                half, ch = divmod(G * k, P // 2)
                carry_m[gi] = pool.mark(pool.q.tensor_copy(
                    first, h[:, half_slot(c - 1, half), ch:ch + G, T:T + 1]))
            if gi >= LAG:
                scan(gi - LAG)
            bm = s["bmat"][:, c * T:(c + 1) * T].unsqueeze(1).broadcast_to([P, G, T])
            dst = inp[:, gi % NB, :, 1:W]
            src = bank_x[gi % 2].rearrange("p (j t) -> p j t", t=T)
            if k in ON_POOL:
                act.wait(bx, scan_m.get(gi - NB))
                inp_m[gi] = act.mark(act.q.copy(dst, src))
                pool.wait(inp_m[gi])
                ready_m[gi] = pool.mark(pool.q.tensor_tensor(dst, dst, bm, ALU.mult))
            else:
                dve.wait(bx, scan_m.get(gi - NB))
                inp_m[gi] = ready_m[gi] = dve.mark(dve.q.tensor_tensor(dst, src, bm, ALU.mult))
            for half in range(2):
                e = 2 * gi + half
                act.wait(prod_m[e], scan_m.get(gi - NB), m_decay0)
                exp_m[e] = act.mark(act.q.activation(
                    decay[:, gi % NB, 4 * half:4 * half + 4, 1:W],
                    bank_a[half][:, :].rearrange("p (j t) -> p j t", t=T), ACT.Exp))

        def scan(gi):
            c, k = divmod(gi, GROUPS)
            half, ch = divmod(G * k, P // 2)
            dve.wait(exp_m[2 * gi + 1], ready_m[gi], carry_m[gi], y_m.get(c - 2 if half == 0 else c - 1))
            flat = lambda v: v.rearrange("p g w -> p (g w)")
            scan_m[gi] = dve.mark(dve.q.tensor_tensor_scan(
                out=flat(h[:, half_slot(c, half), ch:ch + G, :]), data0=flat(decay[:, gi % NB, :, :]),
                data1=flat(inp[:, gi % NB, :, :]), initial=0.0, op0=ALU.mult, op1=ALU.add))

        def read_out(c, js):
            if js[0] == 0:
                pe.wait(scan_m[c * GROUPS + GROUPS - 1], y_read.get(c - 1))
                if c % CPB == 0:
                    pe.wait(place_c(c // CPB))
            slot = c % 2
            for j in js:
                for q in range(4):
                    tok = 16 * q + j
                    mov = h[:, slot:3:2 - slot, :, 1 + tok:1 + tok + 65:64].rearrange("p s d t -> p t s d")
                    ins = pe.q.matmul(bank_y[32 * q:32 * q + 32, 0:256].rearrange("p (t s d) -> p t s d", t=2, s=2),
                                      s["cstat"][:, tok, :], mov, start=j == 0, stop=j == 15)
            y_m[c] = pe.mark(ins) if js[-1] == 15 else None
            if y_m[c] is None:
                del y_m[c]

        def finish_a(c):
            act.wait(y_m[c], epi_t.get(c - 1))
            y_read[c] = act.mark(act.q.copy(y_sb[:, :, :].rearrange("p a b -> p (a b)"), bank_y[:, 0:256]))
            pe.wait(y_read[c], z_used[0])
            for th in range(2):
                ins = pe.q.transpose(bank_z[:, th * P:(th + 1) * P], y_sb[:, th, :], s["ident"][:, :])
            epi_t[c] = pe.mark(ins)
            act.wait(epi_t[c], proj_m.get(c - 1))
            for dh in range(DH):
                m = act.mark(act.q.copy(
                    y_t[:, dh, :].rearrange("p (th t) -> p th t", th=2),
                    bank_z[:, 0:256].rearrange("p (th t k) -> p th t k", th=2, k=2)[:, :, :, dh]))
            yt_m[c] = z_used[0] = m

        def finish_b(c):
            pe.wait(yt_m[c], skip_m[c], wo.all(), z_used[0])
            for dh in range(DH):
                pe.q.matmul(bank_z[:, 0:256], y_t[:, dh, :], w_out[:, dh, :], start=dh == 0, stop=False)
                ins = pe.q.matmul(bank_z[:, 0:256], skip[:, c % 2, dh, :], w_out[:, dh, :], start=False, stop=dh == 1)
            proj_m[c] = pe.mark(ins)
            n = Router.N
            dve.wait(proj_m[c], xres_m[c], store_m.get(c - n), router.normed.get(c // n - 1))
            resid_m[c] = z_used[0] = dve.mark(dve.q.tensor_tensor(x1o[:, c % n, :], bank_z[:, 0:256], xres[:, c % 2, :], ALU.add))
            epi[c] = (proj_m[c], resid_m[c])
            act.wait(resid_m[c])
            store_m[c] = x1_st[c % n].dma(act.q.dma_start(s["x1_d"][c * T:(c + 1) * T, :], x1o[:, c % n, :]))
            if c % n == n - 1:
                routing.append(router.steps(c // n, x1o, [resid_m[i] for i in range(c - n + 1, c + 1)], bank_z,
                                            z_used))

        epi_t, yt_m, routing = {}, {}, []

        def advance():
            if routing and next(routing[0], "done") == "done":
                routing.pop(0)
        load(0)
        load(1)
        total = CHUNKS * GROUPS
        for gi in range(total + LAG):
            c, k = divmod(gi, GROUPS)
            if gi < total:
                stream(gi)
            else:
                scan(gi - LAG)
            advance()
            if c >= 1 and gi < total:
                if LAG <= k < LAG + 8:
                    read_out(c - 1, range(2 * (k - LAG), 2 * (k - LAG) + 2))
                while k in (LAG + 8, LAG + 9) and z_used[0] == "written":
                    advance()
                if k == LAG + 8:
                    finish_a(c - 1)
                if k == LAG + 9:
                    finish_b(c - 1)
                if k == LAG + 10 and c + 1 < CHUNKS:
                    load(c + 1)
        c = CHUNKS - 1
        read_out(c, range(16))
        finish_a(c)
        finish_b(c)
        while routing:
            advance()
        act.wait(*(q.all() for q in x1_st))
        pool.wait(router.scattered.all())


def rest(p, a, out, s):
    nc, act = p.nc, p.act
    with ExitStack() as keep:
        sb = lambda name, shape, dt=F32: p.sb(name, shape, dt, keep)
        x1 = sb("x1", [P, TILES, D])
        wts = dict(wq=sb("wq", [P, DH, D]), wkv=sb("wkv", [P, DH, 2 * D]), wo=sb("wo", [P, DH, D]),
                   brow=sb("brow", [P, 3, D]),
                   c_decay_row=sb("dec_row", [P, SEQ]), c_decay_col=sb("dec_col", [P, CPB]), c_mask=sb("mask", [P, P]),
                   w_gu=sb("wgu", [P, 2, DH, FF]), w_down=sb("wd", [P, FT, D]))
        with ExitStack() as ctx:
            expert_steps = experts(p, a, s, ctx)
            m_x1 = p.count("x1ld").dma(act.q.dma_start(x1[:, :, :], s["x1_d"].rearrange("(i p) d -> p i d", p=P)))
            w = p.count("w_rest")
            for name, tile in wts.items():
                m_w = w.dma(act.q.dma_start(tile[tuple(slice(None) for _ in tile.shape)], a[name]))
            expert_steps()
            nc.all_engine_barrier()
        with ExitStack() as ctx:
            second_layer(p, s, ctx, x1, m_x1, wts, m_w, out)


class Router:
    N = 4

    def __init__(self, p, a, ctx, gates, slots, ident, eps, disp_d):
        self.p, self.gates, self.slots, self.ident, self.eps, self.disp_d = p, gates, slots, ident, eps, disp_d
        sb = lambda name, shape, dt=F32: p.sb("r_" + name, shape, dt, ctx)
        e3 = [P, self.N, EXPERTS]
        self.xl = sb("xl", [P, self.N, D])
        self.xt = sb("xt", [P, DH, P])
        self.wg = sb("wg", [P, DH, EXPERTS])
        self.tri_f, self.tri = sb("tri_f", [P, 2, P]), sb("tri", [P, 2, P], BF16)
        self.erow = sb("erow", [P, 2, EXPERTS])
        self.stats, self.mom = sb("stats", [P, self.N, 6]), sb("mom", [P, self.N, 2])
        self.sd, self.rstd = sb("sd", [P, self.N]), sb("rstd", [P, self.N])
        (self.logit, self.prob, self.oh0, self.oh1, self.place, self.kept, self.tmp, self.cum, self.cs,
         self.top) = (sb(n, e3) for n in ("logit", "prob", "oh0", "oh1", "place", "kept", "tmp", "cum", "cs", "top"))
        self.ind = sb("ind", e3, BF16)
        self.top_i = sb("top_i", e3, U32)
        self.top_f = sb("top_f", [P, self.N, 2])
        self.red = sb("red", [P, 3, self.N])
        self.ones = sb("ones", [P, self.N])
        self.before = sb("before", [P, EXPERTS])
        w = p.count("w_route")
        w.dma(p.act.q.dma_start(self.wg[:, :, :], a["w_gate8"]))
        w.dma(p.act.q.dma_start(self.tri_f[:, :, :], a["c_tri"]))
        self.m_w = w.dma(p.act.q.dma_start(self.erow[:, :, :], a["c_erow"]))
        p.pool.wait(self.m_w)
        p.pool.q.memset(self.ones[:, :], 1.0)
        p.pool.q.memset(self.before[:, :], 0.0)
        self.m_const = p.pool.mark(p.pool.q.tensor_copy(self.tri[:, :, :], self.tri_f[:, :, :]))
        self.scattered = p.count("scatter")
        self.normed = {}

    def steps(self, blk, x1, x1_ready, bank, used):
        p, n3 = self.p, self.N * EXPERTS
        pe, act, dve, pool = p.pe, p.act, p.dve, p.pool
        flat = lambda t: t[:, :, :].rearrange("p i e -> p (i e)")
        e3 = [P, self.N, EXPERTS]
        per_tile = lambda t: t.unsqueeze(2).broadcast_to(e3)
        per_expert = lambda t: t.unsqueeze(1).broadcast_to(e3)
        tiles = slice(self.N * blk, self.N * (blk + 1))

        dve.wait(*x1_ready)
        for i in range(self.N):
            m = dve.mark(dve.q.bn_stats(self.stats[:, i, :], x1[:, i, :]))
        yield
        dve.wait(m)
        for i in range(self.N):
            m = dve.mark(dve.q.bn_aggr(self.mom[:, i, :], self.stats[:, i, :]))
        yield
        act.wait(m)
        m = act.mark(act.q.activation(self.sd[:, :], self.mom[:, :, 1], ACT.Sqrt, bias=self.eps[:, 0:1]))
        yield
        yield
        dve.wait(m)
        m = dve.mark(dve.q.reciprocal(self.rstd[:, :], self.sd[:, :]))
        yield
        dve.wait(m, self.scattered.all() if blk else None)
        for i in range(self.N):
            m = dve.mark(dve.q.tensor_scalar(self.xl[:, i, :], x1[:, i, :], self.mom[:, i, 0:1],
                                             self.rstd[:, i:i + 1], ALU.subtract, ALU.mult))
        self.normed[blk] = m_norm = m
        yield
        for i in range(self.N):
            pe.wait(m_norm, self.m_w, used[0])
            for dh in range(DH):
                ins = pe.q.transpose(bank[:, dh * P:(dh + 1) * P], self.xl[:, i, dh * P:(dh + 1) * P], self.ident[:, :])
            m = pe.mark(ins)
            used[0] = "written"
            yield
            act.wait(m)
            m = used[0] = act.mark(act.q.copy(self.xt[:, :, :].rearrange("p h t -> p (h t)"), bank[:, 0:2 * P]))
            yield
            pe.wait(m, used[0])
            for dh in range(DH):
                ins = pe.q.matmul(bank[:, 256:256 + EXPERTS], self.xt[:, dh, :], self.wg[:, dh, :],
                                  start=dh == 0, stop=dh == 1)
            m = pe.mark(ins)
            used[0] = "written"
            yield
            dve.wait(m)
            m = used[0] = dve.mark(dve.q.tensor_copy(self.logit[:, i, :], bank[:, 256:256 + EXPERTS]))

        def v(ins):
            return dve.mark(ins)

        red = self.red
        yield
        dve.wait(m, self.m_const)
        m = v(dve.q.tensor_reduce(red[:, 0, :], self.logit[:, :, :], AX.X, ALU.max))
        yield
        dve.wait(m)
        m = v(dve.q.tensor_tensor(self.logit[:, :, :], self.logit[:, :, :], per_tile(red[:, 0, :]), ALU.subtract))
        yield
        act.wait(m)
        m = act.mark(act.q.activation(self.prob[:, :, :], self.logit[:, :, :], ACT.Exp))
        yield
        dve.wait(m)
        m = v(dve.q.tensor_reduce(red[:, 1, :], self.prob[:, :, :], AX.X, ALU.add))
        yield
        dve.wait(m)
        m = v(dve.q.reciprocal(red[:, 2, :], red[:, 1, :]))
        yield
        dve.wait(m)
        m = v(dve.q.tensor_tensor(self.prob[:, :, :], self.prob[:, :, :], per_tile(red[:, 2, :]), ALU.mult))
        yield
        dve.wait(m)
        for i in range(self.N):
            m = v(dve.q.max(self.top[:, i, :], self.prob[:, i, :]))
        yield
        dve.wait(m)
        for i in range(self.N):
            m = v(dve.q.max_index(self.top_i[:, i, :], self.top[:, i, :], self.prob[:, i, :]))
        yield
        dve.wait(m)
        m = v(dve.q.tensor_copy(self.top_f[:, :, :], self.top_i[:, :, 0:2]))
        yield
        dve.wait(m)
        number, base = per_expert(self.erow[:, 0, :]), per_expert(self.erow[:, 1, :])
        hots = (self.oh0, self.oh1)
        for k in range(2):
            m = v(dve.q.tensor_tensor(hots[k][:, :, :], number, per_tile(self.top_f[:, :, k]), ALU.is_equal))
        yield
        dve.wait(m)
        m = v(dve.q.tensor_tensor(self.ind[:, :, :], self.oh0[:, :, :], self.oh1[:, :, :], ALU.add))
        yield
        pe.wait(m, self.m_const, used[0])
        pe.q.matmul(bank[:, 256:256 + n3], self.tri[:, 0, :], flat(self.ind), start=True, stop=True)
        m = pe.mark(pe.q.matmul(bank[:, 320:320 + n3], self.tri[:, 1, :], flat(self.ind), start=True, stop=True))
        used[0] = "written"
        yield
        dve.wait(m)
        v(dve.q.tensor_copy(flat(self.cs), bank[:, 320:320 + n3]))
        m = used[0] = v(dve.q.tensor_copy(flat(self.place), bank[:, 256:256 + n3]))
        yield
        dve.wait(m)
        for e in range(EXPERTS):
            m = v(dve.q.tensor_tensor_scan(out=self.cum[:, :, e], data0=self.ones[:, :], data1=self.cs[:, :, e],
                                           initial=self.before[:, e:e + 1], op0=ALU.mult, op1=ALU.add))
        yield
        dve.wait(m)
        m2 = v(dve.q.tensor_copy(self.before[:, :], self.cum[:, self.N - 1, :]))
        m = v(dve.q.tensor_tensor(self.tmp[:, :, :], self.cum[:, :, :], self.cs[:, :, :], ALU.subtract))
        yield
        dve.wait(m)
        m = v(dve.q.tensor_tensor(self.place[:, :, :], self.place[:, :, :], self.tmp[:, :, :], ALU.add))
        yield
        dve.wait(m)
        m = v(dve.q.tensor_scalar(self.kept[:, :, :], self.place[:, :, :], float(CAP), None, ALU.is_lt))
        yield
        dve.wait(m)
        m = v(dve.q.tensor_tensor(self.place[:, :, :], self.place[:, :, :], base, ALU.add))
        yield
        for k in range(2):
            dve.wait(m)
            m = v(dve.q.tensor_tensor(self.tmp[:, :, :], hots[k][:, :, :], self.place[:, :, :], ALU.mult))
            yield
            dve.wait(m)
            m = v(dve.q.tensor_reduce(red[:, 0, :], self.tmp[:, :, :], AX.X, ALU.add))
            yield
            dve.wait(m)
            m = v(dve.q.tensor_tensor(self.tmp[:, :, :], hots[k][:, :, :], self.kept[:, :, :], ALU.mult))
            yield
            dve.wait(m)
            m = v(dve.q.tensor_reduce(red[:, 1, :], self.tmp[:, :, :], AX.X, ALU.add))
            yield
            dve.wait(m)
            v(dve.q.tensor_tensor(self.gates[:, k, tiles], self.top[:, :, k], red[:, 1, :], ALU.mult))
            m = v(dve.q.scalar_tensor_tensor(red[:, 2, :], red[:, 0, :], float(-SLOTS), red[:, 1, :], ALU.add,
                                             ALU.mult))
            yield
            dve.wait(m)
            m = v(dve.q.tensor_scalar(self.slots[:, k, tiles], red[:, 2, :], float(SLOTS), None, ALU.add))
            yield
        pool.wait(m)
        for i in range(self.N):
            for k in range(2):
                t = self.N * blk + i
                self.scattered.dma(pool.q.indirect_dma_start(
                    out=self.disp_d, out_offset=bass.IndirectOffsetOnAxis(ap=self.slots[:, k, t:t + 1], axis=0),
                    in_=self.xl[:, i, :], in_offset=None, bounds_check=SLOTS - 1, oob_is_err=False))
                yield


def experts(p, a, s, ctx):
    pe, act, dve, pool, sp = p.pe, p.act, p.dve, p.pool, p.sp
    sb = lambda name, shape, dt=F32: p.sb(name, shape, dt, ctx)
    NW = 2
    w1 = sb("w1", [P, NW, DH, FF])
    w2 = sb("w2", [P, NW, FT, D])
    xd = sb("xd", [P, 2, ST, D])
    xdt = sb("xdt", [P, 2, DH, CAP])
    hid = sb("hid", [P, 2, FT, CAP])
    eo = sb("eo", [P, 2, ST, D])
    ring = p.ring(8)
    w1_ld, w2_ld, xd_ld, eo_st = ([p.count(f"{n}{i}") for i in range(2)] for n in ("w1", "w2", "xd", "eo"))
    half_cap = CAP // 2
    m_w1, m_w2, m_xd, m_xt, m_up, m_down, m_tr, m_store = {}, {}, {}, {}, {}, {}, {}, {}
    hid_m, turn = {}, [0]

    def evacuate(dst, src, b, wait, relu=False):
        turn[0] += 1
        if turn[0] % 2:
            act.wait(*wait)
            m = act.mark(act.q.activation(dst, src, ACT.Relu) if relu else act.q.copy(dst, src))
        else:
            dve.wait(*wait)
            m = dve.mark(dve.q.tensor_scalar(dst, src, 0.0, None, ALU.max) if relu else dve.q.tensor_copy(dst, src))
        ring.read_by(b, m)
        return m

    def load(e):
        if e >= EXPERTS:
            return
        sp.wait(m_tr.get(e - 2))
        m_xd[e] = xd_ld[e % 2].dma(sp.q.dma_start(
            xd[:, e % 2, :, :], s["disp_d"][e * CAP:(e + 1) * CAP, :].rearrange("(s p) d -> p s d", p=P)))
        sp.wait(m_up.get(e - NW))
        m_w1[e] = w1_ld[e % 2].dma(sp.q.dma_start(w1[:, e % NW, :, :], a["w1"][e]))
        sp.wait(m_down.get(e - NW))
        m_w2[e] = w2_ld[e % 2].dma(sp.q.dma_start(w2[:, e % NW, :, :], a["w2"][e]))

    def transposes(e):
        if e >= EXPERTS:
            return
        pe.wait(m_xd[e])
        ms = []
        for dh in range(DH):
            for first, n in ((0, 4), (4, 1)):
                b, bank = ring.take()
                for j in range(n):
                    ins = pe.q.transpose(bank[:, j * P:(j + 1) * P], xd[:, e % 2, first + j, dh * P:(dh + 1) * P],
                                         s["ident"][:, :])
                m = pe.mark(ins)
                ms.append(evacuate(xdt[:, e % 2, dh, first * P:(first + n) * P], bank[:, 0:n * P], b,
                                   (m, m_up.get(e - 2))))
        m_tr[e] = m
        m_xt[e] = ms

    def up(e):
        pe.wait(m_w1[e], *m_xt[e])
        hid_m[e] = []
        for f in range(FT):
            for c in range(2):
                b, bank = ring.take()
                cs = slice(c * half_cap, (c + 1) * half_cap)
                for dh in range(DH):
                    ins = pe.q.matmul(bank[:, 0:half_cap], w1[:, e % NW, dh, f * P:(f + 1) * P],
                                      xdt[:, e % 2, dh, cs], start=dh == 0, stop=dh == 1)
                m = pe.mark(ins)
                hid_m[e].append(evacuate(hid[:, e % 2, f, cs], bank[:, 0:half_cap], b, (m, m_down.get(e - 2)), True))
        m_up[e] = m

    def down(e):
        pe.wait(m_w2[e], *hid_m[e])
        ms = []
        for st in range(ST):
            b, bank = ring.take()
            for f in range(FT):
                ins = pe.q.matmul(bank[:, 0:D], hid[:, e % 2, f, st * P:(st + 1) * P], w2[:, e % NW, f, :],
                                  start=f == 0, stop=f == FT - 1)
            m = pe.mark(ins)
            ms.append(evacuate(eo[:, e % 2, st, :], bank[:, 0:D], b, (m, m_store.get(e - 2))))
        m_down[e] = m
        sp.wait(*ms)
        m_store[e] = eo_st[e % 2].dma(sp.q.dma_start(
            s["eout_d"][e * CAP:(e + 1) * CAP, :].rearrange("(s p) d -> p s d", p=P), eo[:, e % 2, :, :]))

    load(0)
    load(1)

    def run():
        transposes(0)
        for e in range(EXPERTS):
            up(e)
            transposes(e + 1)
            down(e)
            load(e + 2)
        sp.wait(eo_st[0].all(), eo_st[1].all())
    return run


def second_layer(p, s, ctx, x1, m_x1, wts, m_w, out):
    pe, act, dve, pool, sp = p.pe, p.act, p.dve, p.pool, p.sp
    sb = lambda name, shape, dt=F32: p.sb(name, shape, dt, ctx)
    NT = 4
    BLOCKS = TILES // NT
    gates, slots, ident = s["gates"], s["slots"], s["ident"]
    wq, wkv, wo, brow, dec_row, dec_col, mask, wgu, wd = wts.values()
    xb = sb("xb", [P, TILES, D])
    got = sb("got", [P, 2, 2, NT, D])
    xl = sb("xl", [P, 2, NT, D])
    xt = sb("xt", [P, 2, DH, 512])
    qt = sb("qt", [P, 2, TOK])
    kv = sb("kv", [P, 2, 2, D])
    va = sb("va", [P, 2, 2, P + 1])
    bd = sb("bd", [P, 2, P])
    kden = sb("kden", [P, 2, P])
    den = sb("den", [P, 2, 512])
    at = sb("at", [P, 2, 2, 512])
    sil = sb("sil", [P, 2, 512])
    gt = sb("gt", [P, 2, FT, 512])
    o = sb("o", [P, 2, NT, D])
    norms = [dict(stats=sb(f"stats{n}", [P, TILES, 6]), mom=sb(f"mom{n}", [P, TILES, 2]), sd=sb(f"sd{n}", [P, TILES]),
                  rstd=sb(f"rstd{n}", [P, TILES]), eps=s["eps"]) for n in range(2)]
    ring = p.ring(6)
    bank_kv = p.banks[6:8]
    m_ones = pool.mark(pool.q.memset(va[:, :, :, P:P + 1], 1.0))
    for e in (pe, act, dve, pool):
        e.wait(m_w)
    dve.wait(m_x1, m_ones)
    tiles_of = lambda blk: list(range(NT * blk, NT * (blk + 1)))
    got_free, x2_m, x2b_m, x3_m = {}, {}, {}, {}
    xl_free, xt_free, xl_use, xl_m, xt_m = {}, {}, [0], {}, {}
    q_m, kv_free, at_m, at_free, gt_m, gt_free, sil_free, down_m = {}, {}, {}, {}, {}, {}, {}, {}
    bd_m, kv_read = {}, []
    out_v = out.rearrange("b (i p) d -> p (b i) d", p=P)
    st = [p.count(f"out{i}") for i in range(2)]

    def gather(blk):
        c = p.count(f"gather{blk}")
        pool.wait(*got_free.get(blk - 2, ()))
        for n, i in enumerate(tiles_of(blk)):
            for k in range(2):
                m = c.dma(pool.q.indirect_dma_start(
                    out=got[:, blk % 2, k, n, :], out_offset=None, in_=s["eout_d"],
                    in_offset=bass.IndirectOffsetOnAxis(ap=slots[:, k, i:i + 1], axis=0)))
        return m

    def combine(blk, m_rows):
        dve.wait(m_rows)
        first = {}
        for n, i in enumerate(tiles_of(blk)):
            first[i] = dve.mark(dve.q.scalar_tensor_tensor(xb[:, i, :], got[:, blk % 2, 0, n, :], gates[:, 0, i:i + 1],
                                                           x1[:, i, :], ALU.mult, ALU.add))
        for n, i in enumerate(tiles_of(blk)):
            dve.wait(first[i])
            x2_m[i] = dve.mark(dve.q.scalar_tensor_tensor(xb[:, i, :], got[:, blk % 2, 1, n, :], gates[:, 1, i:i + 1],
                                                          xb[:, i, :], ALU.mult, ALU.add))
        got_free[blk] = (x2_m[i],)

    def add_bias(blk):
        for i in tiles_of(blk):
            pool.wait(x2_m[i])
            x2b_m[i] = pool.mark(pool.q.tensor_tensor(x1[:, i, :], xb[:, i, :], brow[:, 2, :], ALU.add))

    def norm(key, blk, which, ready):
        tiles = tiles_of(blk)
        layer_norm_stats(p, xb, tiles, src_ready=ready, **norms[which])
        u = xl_use[0] % 2
        xl_use[0] += 1
        dve.wait(xl_free.get(u))
        for n, i in enumerate(tiles):
            m = dve.mark(dve.q.tensor_scalar(xl[:, u, n, :], xb[:, i, :], norms[which]["mom"][:, i, 0:1],
                                             norms[which]["rstd"][:, i:i + 1], ALU.subtract, ALU.mult))
        xl_m[key] = (u, m)

    def transposes(key):
        u, m = xl_m[key]
        pe.wait(m)
        ms = []
        for dh in range(DH):
            bk, bank = ring.take()
            for n in range(NT):
                ins = pe.q.transpose(bank[:, n * P:(n + 1) * P], xl[:, u, n, dh * P:(dh + 1) * P], ident[:, :])
            m = pe.mark(ins)
            act.wait(m, xt_free.get(u))
            ms.append(act.mark(act.q.copy(xt[:, u, dh, :], bank[:, :])))
            ring.read_by(bk, ms[-1])
        xl_free[u] = m
        xt_m[key] = (u, ms)

    def project_qkv(blk):
        u, ms = xt_m["a", blk]
        pe.wait(*ms)
        t5 = slice(512 * blk, 512 * (blk + 1))
        for hh in range(2):
            bk, bank = ring.take()
            for dh in range(DH):
                ins = pe.q.matmul(bank[:, :], wq[:, dh, hh * P:(hh + 1) * P], xt[:, u, dh, :],
                                  start=dh == 0, stop=dh == 1)
            m = pe.mark(ins)
            act.wait(m)
            m = act.mark(act.q.activation(qt[:, hh, t5], bank[:, :], ACT.Relu, bias=s["bq"][:, hh:hh + 1]))
            ring.read_by(bk, m)
            pool.wait(m)
            pos = 512 * blk % SEQ
            q_m[blk, hh] = pool.mark(pool.q.tensor_tensor(qt[:, hh, t5], qt[:, hh, t5], dec_row[:, pos:pos + 512],
                                                          ALU.mult))
        kv_m = {}
        for n, i in enumerate(tiles_of(blk) + [None]):
            if i is not None:
                bk, bank = ring.take()
                for dh in range(DH):
                    ins = pe.q.matmul(bank[:, :], xt[:, u, dh, n * P:(n + 1) * P], wkv[:, dh, :],
                                      start=dh == 0, stop=dh == 1)
                m = pe.mark(ins)
                w = i % 2
                dve.wait(m, kv_free.get(w))
                m1 = dve.mark(dve.q.tensor_tensor(kv[:, w, 0, :], bank[:, 0:D], brow[:, 0, :], ALU.add))
                m2 = dve.mark(dve.q.tensor_tensor(
                    va[:, w, :, 0:P], bank[:, D:2 * D].rearrange("p (h e) -> p h e", h=2),
                    brow[:, 1, :].rearrange("p (h e) -> p h e", h=2), ALU.add))
                ring.read_by(bk, m2)
                dve.wait(m1)
                kv_m[i] = dve.mark(dve.q.tensor_scalar(kv[:, w, 1, :], kv[:, w, 0, :], 0.0,
                                                       dec_col[:, i % CPB:i % CPB + 1], ALU.max, ALU.mult))
                xt_free[u] = m
            if n:
                j = NT * blk + n - 1
                w = j % 2
                pe.wait(kv_m[j], *kv_read)
                for hh in range(2):
                    ins = pe.q.matmul(bank_kv[hh][:, 0:P + 1], kv[:, w, 1, hh * P:(hh + 1) * P], va[:, w, hh, :],
                                      start=j % CPB == 0, stop=j % CPB == CPB - 1)
                kv_free[w] = pe.mark(ins)

    def heads(b):
        dve.wait(kv_free[1], bd_m.get("used"))
        for hh in range(2):
            dve.mark(dve.q.tensor_tensor(bd[:, hh, :], bank_kv[hh][:, 0:P], mask[:, :], ALU.mult))
            m = dve.mark(dve.q.tensor_scalar(kden[:, hh, :], mask[:, :], bank_kv[hh][:, P:P + 1], None, ALU.mult))
        bd_m["m"] = m
        kv_read[:] = [m]

    def attend(blk):
        t5 = slice(512 * blk, 512 * (blk + 1))
        pe.wait(bd_m["m"])
        at_m[blk] = []
        for hh in range(2):
            pe.wait(q_m[blk, hh])
            bk1, bank1 = ring.take()
            m1 = pe.mark(pe.q.matmul(bank1[:, :], kden[:, hh, :], qt[:, hh, t5], start=True, stop=True))
            bk2, bank2 = ring.take()
            m2 = bd_m["used"] = pe.mark(pe.q.matmul(bank2[:, :], bd[:, hh, :], qt[:, hh, t5], start=True, stop=True))
            dve.wait(m1)
            m = dve.mark(dve.q.tensor_scalar(den[:, hh, :], bank1[:, :], 1e-6, None, ALU.add))
            ring.read_by(bk1, m)
            dve.wait(m)
            m = dve.mark(dve.q.reciprocal(den[:, hh, :], den[:, hh, :]))
            dve.wait(m, m2, at_free.get(blk % 2))
            m = dve.mark(dve.q.tensor_tensor(at[:, blk % 2, hh, :], bank2[:, :], den[:, hh, :], ALU.mult))
            ring.read_by(bk2, m)
            at_m[blk].append(m)

    def attention_out(blk):
        pe.wait(*at_m[blk])
        for n, i in enumerate(tiles_of(blk)):
            bk, bank = ring.take()
            for hh in range(2):
                ins = pe.q.matmul(bank[:, 0:D], at[:, blk % 2, hh, n * P:(n + 1) * P], wo[:, hh, :],
                                  start=hh == 0, stop=hh == 1)
            m = at_free[blk % 2] = pe.mark(ins)
            dve.wait(m, x2b_m[i])
            x3_m[i] = dve.mark(dve.q.tensor_tensor(xb[:, i, :], bank[:, 0:D], x1[:, i, :], ALU.add))
            ring.read_by(bk, x3_m[i])

    def gate_up(blk):
        u, ms = xt_m["m", blk]
        pe.wait(*ms)
        gt_m[blk] = []
        for f in range(FT):
            pair = []
            for j in range(2):
                bk, bank = ring.take()
                for dh in range(DH):
                    ins = pe.q.matmul(bank[:, :], wgu[:, j, dh, f * P:(f + 1) * P], xt[:, u, dh, :],
                                      start=dh == 0, stop=dh == 1)
                pair.append((bk, bank, pe.mark(ins)))
            w = f % 2
            act.wait(pair[0][2], sil_free.get(w))
            m = act.mark(act.q.activation(sil[:, w, :], pair[0][1][:, :], ACT.Silu))
            ring.read_by(pair[0][0], m)
            dve.wait(m, pair[1][2], gt_free.get(blk % 2))
            m = dve.mark(dve.q.tensor_tensor(gt[:, blk % 2, f, :], pair[1][1][:, :], sil[:, w, :], ALU.mult))
            ring.read_by(pair[1][0], m)
            sil_free[w] = m
            gt_m[blk].append(m)
        xt_free[u] = pair[1][2]

    def down(blk):
        pe.wait(*gt_m[blk])
        for n, i in enumerate(tiles_of(blk)):
            bk, bank = ring.take()
            for f in range(FT):
                ins = pe.q.matmul(bank[:, 0:D], gt[:, blk % 2, f, n * P:(n + 1) * P], wd[:, f, :],
                                  start=f == 0, stop=f == FT - 1)
            m = pe.mark(ins)
            dve.wait(m, down_m.get(blk - 2))
            mo = dve.mark(dve.q.tensor_tensor(o[:, blk % 2, n, :], bank[:, 0:D], xb[:, i, :], ALU.add))
            ring.read_by(bk, mo)
            if n % 2:
                sp.wait(mo)
                stored = st[blk % 2].dma(sp.q.dma_start(out_v[:, i - 1:i + 1, :], o[:, blk % 2, n - 1:n + 1, :]))
        gt_free[blk % 2] = m
        down_m[blk] = stored

    def ready(blk):
        combine(blk, rows[blk])
        norm(("a", blk), blk, 0, x2_m)

    rows = {0: gather(0), 1: gather(1)}
    ready(0)
    ready(1)
    transposes(("a", 0))
    project_qkv(0)
    transposes(("a", 1))
    for blk in (2, 3):
        rows[blk] = gather(blk)
    project_qkv(1)
    for blk in range(2):
        add_bias(blk)
    heads(0)
    attend(0)
    ready(2)
    attend(1)
    attention_out(0)
    transposes(("a", 2))
    attention_out(1)
    ready(3)
    project_qkv(2)
    transposes(("a", 3))
    norm(("m", 0), 0, 1, x3_m)
    project_qkv(3)
    for blk in range(2, 4):
        add_bias(blk)
    heads(1)
    transposes(("m", 0))
    attend(2)
    attend(3)
    norm(("m", 1), 1, 1, x3_m)
    attention_out(2)
    attention_out(3)
    for blk in range(BLOCKS):
        gate_up(blk)
        if blk + 1 < BLOCKS:
            transposes(("m", blk + 1))
        if blk + 2 < BLOCKS:
            norm(("m", blk + 2), blk + 2, 1, x3_m)
        down(blk)
    sp.wait(st[0].all(), st[1].all())


def lay_out(v):
    f = np.ascontiguousarray
    halves_t = lambda w: w.T.reshape(DH, P, w.shape[0]).transpose(1, 0, 2)
    col = lambda w: w.reshape(DH, P).T
    xp = v["L0_attn_x_proj_w"]
    dt_w, b_w, c_w = xp[:RANK], xp[RANK:RANK + STATE], xp[RANK + STATE:]
    proj = np.concatenate([dt_w, b_w, b_w, c_w, c_w])
    sel = np.zeros((P, ROWG, P), np.float32)
    for g in range(ROWG):
        for r in range(6, 12):
            sel[32 * g + r, g, STATE * (r % 2):STATE * (r % 2) + STATE] = 1
    z = {
        "x": v["L0_attn_x"],
        "c_ident": np.eye(P, dtype=np.float32),
        "c_sel": sel,
        "cols": np.stack([col(v[n]) for n in ("L0_attn_norm_w", "L0_attn_norm_b", "L0_attn_D_param",
                                              "L0_attn_dt_proj_b", "L1_attn_bq", "L1_attn_bk", "L1_attn_bv")], 1),
        "w_proj": halves_t(proj).reshape(P, DH, 3, P),
        "w_dt": v["L0_attn_dt_proj_w"].T,
        "a_log": v["L0_attn_A_log"].reshape(DH, P, STATE).transpose(1, 0, 2),
        "w_out": halves_t(v["L0_attn_out_proj_w"]),
    }
    pos = np.arange(SEQ, dtype=np.float32)
    decay = np.exp(-pos / np.float32(SEQ)).astype(np.float32)
    head = np.arange(P) // DK
    bk, bv, bo = (v["L1_attn_" + n] for n in ("bk", "bv", "bo"))
    z |= {
        "c_tri": np.stack([np.triu(np.ones((P, P)), 1), np.ones((P, P))], 1).astype(np.float32),
        "c_erow": np.broadcast_to(np.stack([np.arange(EXPERTS), CAP * np.arange(EXPERTS)]).astype(np.float32),
                                  (P, 2, EXPERTS)),
        "c_decay_row": np.broadcast_to(decay, (P, SEQ)),
        "c_decay_col": decay.reshape(CPB, P).T,
        "c_mask": (head[:, None] == head[None, :]).astype(np.float32),
        "w_gate8": v["L0_ffn_Wg"].reshape(DH, P, EXPERTS).transpose(1, 0, 2),
        "w1": v["L0_ffn_w1"].reshape(EXPERTS, DH, P, FF).transpose(0, 2, 1, 3),
        "w2": v["L0_ffn_w2"].reshape(EXPERTS, FT, P, D).transpose(0, 2, 1, 3),
        "wq": halves_t(v["L1_attn_Wq"]),
        "wkv": halves_t(np.concatenate([v["L1_attn_Wk"], v["L1_attn_Wv"]])),
        "wo": halves_t(v["L1_attn_Wo"]),
        "brow": np.broadcast_to(np.stack([bk, bv, bo]), (P, 3, D)),
        "w_gu": np.stack([halves_t(v["L1_ffn_w_gate"]), halves_t(v["L1_ffn_w_up"])], 1),
        "w_down": v["L1_ffn_w_down"].T.reshape(FT, P, D).transpose(1, 0, 2),
    }
    return {k: f(x) for k, x in z.items()}


def kernel(**inputs):
    import concourse.bacc as bacc
    from concourse.bass_utils import run_bass_kernel_spmd
    arrays = lay_out({k: np.asarray(v) for k, v in inputs.items()})
    nc = bacc.Bacc("TRN2", target_bir_lowering=False, num_devices=1)
    aps = {k: nc.dram_tensor("in_" + k, x.shape, mybir.dt.from_np(x.dtype), kind="ExternalInput").ap()
           for k, x in arrays.items()}
    out = nc.dram_tensor("out", [BATCH, SEQ, D], F32, kind="ExternalOutput").ap()
    build(nc, aps, out)
    r = run_bass_kernel_spmd(nc, [{"in_" + k: x for k, x in arrays.items()}], core_ids=[0])
    return r.results[0]["out"]
```

```python
from math import gcd
from contextlib import ExitStack

import numpy as np
import concourse.bass as bass
from concourse import mybir

P = 128
F32 = mybir.dt.float32
BF16 = mybir.dt.bfloat16
U32 = mybir.dt.uint32
ALU = mybir.AluOpType
ACT = mybir.ActivationFunctionType
AX = mybir.AxisListType

BATCH, SEQ, D = 2, 1024, 256
TOK = BATCH * SEQ
TILES = TOK // P
DH = D // P
RANK, STATE, CSPAN = 128, 64, 64
EXPERTS, FF = 8, 1024
CAP = -(-5 * TOK * 2 // (4 * EXPERTS))
SLOTS = EXPERTS * CAP
ST = CAP // P
FT = FF // P
HEADS, DK = 16, 16
EPS = 1e-5

T = 128
CHUNKS = TOK // T
CPB = SEQ // T
G = 8
GROUPS = P // G
ROWG = 4
RCH = P // ROWG
LAG = 2
ON_POOL = (1, 3, 5, 8, 10, 12, 15)
W = T + 1


class Mark:

    def __init__(self, sem, value):
        self.sem, self.value = sem, value


class Count:

    def __init__(self, sem):
        self.sem, self.n = sem, 0

    def up(self, ins, by):
        self.n += by
        ins.then_inc(self.sem, by)
        return Mark(self.sem, self.n)

    def dma(self, ins):
        return self.up(ins, 16)

    def all(self):
        return Mark(self.sem, self.n)


class Engine:

    def __init__(self, queue, sem):
        self.q, self.count, self.met = queue, Count(sem), {}

    def mark(self, ins):
        return self.count.up(ins, 1)

    def wait(self, *marks):
        for m in marks:
            if m is not None and m.value > self.met.get(id(m.sem), 0):
                self.q.wait_ge(m.sem, m.value)
                self.met[id(m.sem)] = m.value


class Program:
    def __init__(self, nc, ctx):
        self.nc, self.ctx = nc, ctx
        self.pe = Engine(nc.tensor, self.sem("pe"))
        self.act = Engine(nc.scalar, self.sem("act"))
        self.dve = Engine(nc.vector, self.sem("dve"))
        self.pool = Engine(nc.gpsimd, self.sem("pool"))
        self.sp = Engine(nc.sync, self.sem("sp"))
        self.psum = ctx.enter_context(nc.psum_tensor("psum", [P, 8 * 512], F32))
        self.banks = [self.psum[:, 512 * i:512 * (i + 1)] for i in range(8)]

    def sem(self, name):
        return self.ctx.enter_context(self.nc.semaphore("s_" + name))

    def count(self, name):
        return Count(self.sem(name))

    def sb(self, name, shape, dt=F32, ctx=None):
        return (ctx or self.ctx).enter_context(self.nc.sbuf_tensor(name, shape, dt))

    def dram(self, name, shape, dt=F32):
        return self.nc.dram_tensor(name, shape, dt).ap()

    def ring(self, n, first=0):
        return Banks(self, list(range(first, first + n)))


class Banks:
    def __init__(self, p, which):
        self.p, self.which, self.at, self.free = p, which, 0, {}

    def take(self):
        b = self.which[self.at % len(self.which)]
        self.at += 1
        self.p.pe.wait(*self.free.get(b, ()))
        return b, self.p.banks[b]

    def read_by(self, b, *marks):
        self.free[b] = marks


def layer_norm_stats(p, src, tiles, stats, mom, sd, rstd, eps, src_ready):
    dve, act = p.dve, p.act
    for i in tiles:
        dve.wait(src_ready[i])
        m = dve.mark(dve.q.bn_stats(stats[:, i, :], src[:, i, :]))
    dve.wait(m)
    for i in tiles:
        m = dve.mark(dve.q.bn_aggr(mom[:, i, :], stats[:, i, :]))
    a, b = tiles[0], tiles[-1] + 1
    act.wait(m)
    m = act.mark(act.q.activation(sd[:, a:b], mom[:, a:b, 1], ACT.Sqrt, bias=eps[:, 0:1]))
    dve.wait(m)
    m = dve.mark(dve.q.reciprocal(rstd[:, a:b], sd[:, a:b]))
    dve.wait(m)


def normalize(p, dst, src, tiles, mom, rstd):
    dve = p.dve
    return {i: dve.mark(dve.q.tensor_scalar(dst[:, i, :], src[:, i, :], mom[:, i, 0:1], rstd[:, i:i + 1],
                                            ALU.subtract, ALU.mult)) for i in tiles}


def transpose_block(p, ring, src, ready, tiles, dh, ident):
    pe = p.pe
    b, bank = ring.take()
    for n, i in enumerate(tiles):
        pe.wait(ready[i])
        ins = pe.q.transpose(bank[:, n * P:(n + 1) * P], src[:, i, dh * P:(dh + 1) * P], ident[:, :])
    return b, bank, pe.mark(ins)


def build(nc, a, out):
    with ExitStack() as ctx:
        p = Program(nc, ctx)
        pe, act, dve, pool, sp = p.pe, p.act, p.dve, p.pool, p.sp

        parts_d = p.dram("parts_d", [CHUNKS, 6, DH, P, T], BF16)
        decay_parts_d = p.dram("decay_parts_d", [3, DH, P, STATE], BF16)
        skip_d = p.dram("skip_d", [P, DH, TOK])
        x1_d = p.dram("x1_d", [TOK, D])
        disp_d = p.dram("disp_d", [SLOTS + 1, D])
        eout_d = p.dram("eout_d", [SLOTS + 1, D])

        ident = p.sb("ident", [P, P])
        cols = p.sb("cols", [P, 5, DH])
        eps = p.sb("eps", [P, 1])
        gates = p.sb("gates", [P, 2, TILES])
        slots = p.sb("slots", [P, 2, TILES], U32)
        shared = p.sb("shared", [P, P * P // 2])
        one = p.sb("one", [P, 1])
        consts = p.count("consts")
        consts.dma(sp.q.dma_start(ident[:, :], a["c_ident"]))
        m_const = consts.dma(sp.q.dma_start(cols[:, :, :], a["cols"]))
        norm_w, norm_b, skip_w, dt_b, bq = (cols[:, i, :] for i in range(5))
        pool.q.memset(eps[:, :], EPS)
        m_eps = pool.mark(pool.q.memset(one[:, :], 1.0))

        with ExitStack() as scan_ctx:
            sb = lambda name, shape, dt=F32: p.sb(name, shape, dt, scan_ctx)
            bmat = sb("bmat", [P, TOK])
            cmat = sb("cmat", [P, BATCH, CSPAN])
            cstat = sb("cstat", [P, CSPAN, 32])
            astat = shared[:, :].bitcast(BF16).rearrange("p (c m) -> p c m", m=P)
            rows = sb("rows", [P, 2, RCH, T], BF16)
            rows_ld = [p.count(f"rows{i}") for i in range(2)]
            w_ld = [p.count(f"w_expert{i}") for i in range(2)]
            sel = sb("sel", [P, ROWG, P], BF16)
            m_rows = prepare(p, a, dict(ident=ident, norm_w=norm_w, norm_b=norm_b, skip_w=skip_w, dt_b=dt_b, eps=eps,
                               one=one, bmat=bmat, cmat=cmat, cstat=cstat, astat=astat, sel=sel, rows=rows, rows_ld=rows_ld, m_const=m_const, m_eps=m_eps,
                               parts_d=parts_d, decay_parts_d=decay_parts_d, skip_d=skip_d, disp_d=disp_d,
                               eout_d=eout_d))
            nc.all_engine_barrier()
            selective_scan(p, a, dict(ident=ident, bmat=bmat, cstat=cstat, astat=astat, sel=sel,
                                      parts_d=parts_d, skip_d=skip_d, x1_d=x1_d, cmat=cmat, eps=eps,
                                      disp_d=disp_d, gates=gates, slots=slots, rows=rows, rows_ld=rows_ld,
                                      m_rows=m_rows, w12=expert_weights(shared), w_ld=w_ld))
            nc.all_engine_barrier()
        rest(p, a, out, dict(shared=shared, w_ld=w_ld, gates=gates, slots=slots, ident=ident, bq=bq, eps=eps, one=one, x1_d=x1_d, disp_d=disp_d, eout_d=eout_d))


def expert_weights(shared):
    half = P * P // 4
    return (shared[:, 0:half].rearrange("p (e h f) -> p e h f", e=2, h=DH),
            shared[:, half:].rearrange("p (e f d) -> p e f d", e=2, f=FT))


def split3(p, v, hi, mid, lo, rest, free):
    act, dve = p.act, p.dve
    m = act.mark(act.q.copy(hi, v))
    dve.wait(m, *free)
    m = dve.mark(dve.q.tensor_tensor(rest, v, hi, ALU.subtract))
    act.wait(m)
    m = act.mark(act.q.copy(mid, rest))
    dve.wait(m)
    return dve.mark(dve.q.tensor_tensor(lo, rest, mid, ALU.subtract))


def prepare(p, a, s):
    pe, act, dve, pool, sp = p.pe, p.act, p.dve, p.pool, p.sp
    ident = s["ident"]
    with ExitStack() as ctx:
        sb = lambda name, shape, dt=F32: p.sb(name, shape, dt, ctx)
        xa = sb("xa", [P, TILES, D])
        x1 = sb("x1n", [P, TILES, D])
        xn_t = sb("xn_t", [P, DH, TOK])
        skip = sb("skip", [P, 2, DH, 512])
        w_proj = sb("w_proj", [P, DH, 3, P])
        w_dt = sb("w_dt", [P, D])
        delta = sb("delta", [P, 2, 512])
        sp_e = sb("sp_e", [P, DH, TOK])
        sp_r = sb("sp_r", [P, DH, TOK])
        parts = sb("parts", [P, 2, 6, DH, 512], BF16)
        rest = sb("rest", [P, 2, DH, 512])
        stats = sb("stats", [P, TILES, 6])
        mom = sb("mom", [P, TILES, 2])
        sd = sb("sd", [P, TILES])
        rstd = sb("rstd", [P, TILES])
        a_sb = sb("a_sb", [P, DH, STATE])
        sel_f = sb("sel_f", [P, ROWG, P])
        a_rest = sb("a_rest", [P, DH, STATE])
        a_parts = sb("a_parts", [P, 3, DH, STATE], BF16)

        x_in = a["x"].rearrange("b (i p) d -> p (b i) d", p=P)
        x_ready = {}
        for blk in range(4):
            c = p.count(f"x{blk}")
            m = c.dma(sp.q.dma_start(xa[:, 4 * blk:4 * blk + 4, :], x_in[:, 4 * blk:4 * blk + 4, :]))
            x_ready.update({i: m for i in range(4 * blk, 4 * blk + 4)})
        weights = p.count("w0")
        weights.dma(act.q.dma_start(w_proj[:, :, :, :], a["w_proj"]))
        weights.dma(act.q.dma_start(w_dt[:, :], a["w_dt"]))
        m_w = weights.dma(act.q.dma_start(a_sb[:, :, :], a["a_log"]))
        selc = p.count("selc")
        m_sel = selc.dma(act.q.dma_start(sel_f[:, :, :], a["c_sel"]))

        zero = s["rows"][:, :, :, :].bitcast(F32).rearrange("p c r t -> p (c r t)")
        m_zero = pool.mark(pool.q.memset(zero, 0.0))
        pool.q.memset(s["cstat"][:, :, :], 0.0)
        m_a0 = pool.mark(pool.q.memset(s["astat"][:, :, :].bitcast(F32), 0.0))
        pool.wait(m_sel)
        pool.q.tensor_copy(s["sel"][:, :, :], sel_f[:, :, :])
        zeros = p.count("zeros")
        sp.wait(m_zero)
        zero_rows = gcd(SLOTS, RCH * T // D * P)
        for r in range(0, SLOTS, zero_rows):
            zeros.dma(sp.q.dma_start(s["disp_d"][r:r + zero_rows, :].rearrange("(p r) d -> p (r d)", p=P),
                                     zero[:, 0:zero_rows // P * D]))
        m_zeros = zeros.dma(sp.q.dma_start(s["eout_d"][SLOTS:SLOTS + 1, :], zero[0:1, 0:D]))

        act.wait(m_w)
        m = act.mark(act.q.activation(a_sb[:, :, :], a_sb[:, :, :], ACT.Exp))
        act.wait(m)
        m = act.mark(act.q.mul(a_sb[:, :, :], a_sb[:, :, :], -1.0))
        act.wait(m)
        m = split3(p, a_sb[:, :, :], a_parts[:, 0, :, :], a_parts[:, 1, :, :], a_parts[:, 2, :, :],
                   a_rest[:, :, :], [m])
        aw = p.count("aw")
        pool.wait(m)
        for k in range(3):
            m = aw.dma(pool.q.dma_start(s["decay_parts_d"][k].rearrange("h p n -> p h n"), a_parts[:, k, :, :]))
        pool.wait(m, m_a0)
        al = p.count("al")
        for g in range(ROWG):
            for dh in range(DH):
                for k, (first, n) in enumerate(((0, 3), (12, 2), (16, 1))):
                    row = 32 * g + first + dh
                    al.dma(pool.q.dma_start(
                        s["astat"][row:row + 2 * n - 1:2, RCH * g:RCH * (g + 1), dh * STATE:(dh + 1) * STATE],
                        s["decay_parts_d"][k:k + 1, dh, RCH * g:RCH * (g + 1), :].broadcast_to([n, RCH, STATE])))

        every = list(range(TILES))
        x1_ready, xh_ready = {}, {}
        act.wait(s["m_eps"])

        def norms(blk):
            tiles = every[4 * blk:4 * blk + 4]
            layer_norm_stats(p, xa, tiles, stats, mom, sd, rstd, s["eps"], x_ready)
            x1_ready.update(normalize(p, x1, xa, tiles, mom, rstd))
            layer_norm_stats(p, x1, tiles, stats, mom, sd, rstd, s["eps"], x1_ready)
            xh_ready.update(normalize(p, xa, x1, tiles, mom, rstd))

        ring = p.ring(8)
        pe.wait(s["m_const"], weights.all())
        act.wait(s["m_const"], s["m_eps"])
        dve.wait(s["m_const"])
        delta_free, parts_free, rest_free = {}, {}, {}
        zs, skip_m, stores = {}, {}, {}
        spill = [p.count(f"spill{i}") for i in range(2)]
        spilled, m_rows = {}, {}
        spill_parts = [p.count(f"spill_parts{i}") for i in range(2)]
        xn_ms, e_m, r_m = {}, {}, {}
        m_parts0 = None

        def project(blk):
            tiles = every[4 * blk:4 * blk + 4]
            t5 = slice(512 * blk, 512 * blk + 512)
            xn_m = xn_ms[blk] = []
            for dh in range(DH):
                b, bank, m = transpose_block(p, ring, xa, xh_ready, tiles, dh, ident)
                act.wait(m)
                m = act.mark(act.q.activation(xn_t[:, dh, t5], bank[:, :], ACT.Identity,
                                              bias=s["norm_b"][:, dh:dh + 1], scale=s["norm_w"][:, dh:dh + 1]))
                ring.read_by(b, m)
                xn_m.append(m)
                b, bank, m = transpose_block(p, ring, x1, x1_ready, tiles, dh, ident)
                dve.wait(m, spilled.get(blk - 2))
                m = dve.mark(dve.q.tensor_scalar(skip[:, blk % 2, dh, :], bank[:, :], s["skip_w"][:, dh:dh + 1], None,
                                                 ALU.mult))
                ring.read_by(b, m)
                sp.wait(m)
                m_spill = spill[blk % 2].dma(sp.q.dma_start(s["skip_d"][:, dh, t5], skip[:, blk % 2, dh, :]))
            spilled[blk] = m_spill
            pe.wait(*xn_m)
            for j in range(2):
                b, bank = ring.take()
                for dh in range(DH):
                    ins = pe.q.matmul(bank[:, :], w_proj[:, dh, j, :], xn_t[:, dh, t5], start=dh == 0, stop=dh == 1)
                m = pe.mark(ins)
                act.wait(m, delta_free.get(blk % 2) if j == 0 else None)
                dst = delta[:, blk % 2, :] if j == 0 else s["bmat"][:, t5]
                m = act.mark(act.q.copy(dst, bank[:, :]))
                ring.read_by(b, m)
                if j == 0:
                    m_delta = m
            if blk % 2 == 0:
                b, bank = ring.take()
                for dh in range(DH):
                    ins = pe.q.matmul(bank[:, 0:CSPAN], w_proj[:, dh, 2, :], xn_t[:, dh, 512 * blk:512 * blk + CSPAN],
                                      start=dh == 0, stop=dh == 1)
                m = pe.mark(ins)
                act.wait(m)
                m = act.mark(act.q.copy(s["cmat"][:, blk // 2, :], bank[:, 0:CSPAN]))
                ring.read_by(b, m)
            pe.wait(m_delta)
            for dh in range(DH):
                b, bank = ring.take()
                m = pe.mark(pe.q.matmul(bank[:, :], w_dt[:, dh * P:(dh + 1) * P], delta[:, blk % 2, :],
                                        start=True, stop=True))
                act.wait(m)
                ma = act.mark(act.q.activation(sp_e[:, dh, t5], bank[:, :], ACT.Abs, bias=s["dt_b"][:, dh:dh + 1]))
                dve.wait(ma)
                mr = dve.mark(dve.q.tensor_scalar(sp_r[:, dh, t5], bank[:, :], s["dt_b"][:, dh:dh + 1], 0.0,
                                                  ALU.add, ALU.max))
                ring.read_by(b, ma, mr)
            delta_free[blk % 2] = m
            e_m[blk], r_m[blk] = ma, mr

        def split(blk):
            nonlocal m_parts0
            t5 = slice(512 * blk, 512 * blk + 512)
            act.wait(e_m[blk])
            m = act.mark(act.q.activation(sp_e[:, :, t5], sp_e[:, :, t5], ACT.Exp, scale=-1.0))
            act.wait(m)
            m = act.mark(act.q.activation(sp_e[:, :, t5], sp_e[:, :, t5], ACT.Ln, bias=s["one"][:, 0:1]))
            dve.wait(m, r_m[blk], *xn_ms[blk])
            m_dt = dve.mark(dve.q.tensor_tensor(sp_e[:, :, t5], sp_e[:, :, t5], sp_r[:, :, t5], ALU.add))
            dve.wait(m_dt)
            m_dtx = dve.mark(dve.q.tensor_tensor(sp_r[:, :, t5], sp_e[:, :, t5], xn_t[:, :, t5], ALU.mult))
            act.wait(m_dt, *stores.get(blk % 2, ()))
            dve.wait(*stores.get(blk % 2, ()))
            part = lambda n, k: parts[:, blk % 2, 3 * n + k, :, :]
            vs, m_v = (sp_e[:, :, t5], sp_r[:, :, t5]), (m_dt, m_dtx)
            m_hi, m_rest, m_mid, done = {}, {}, {}, []
            for n in range(2):
                act.wait(m_v[n])
                m_hi[n] = act.mark(act.q.copy(part(n, 0), vs[n]))
            for n in range(2):
                dve.wait(m_hi[n], rest_free.get(n))
                m_rest[n] = dve.mark(dve.q.tensor_tensor(rest[:, n, :, :], vs[n], part(n, 0), ALU.subtract))
            for n in range(2):
                act.wait(m_rest[n])
                m_mid[n] = act.mark(act.q.copy(part(n, 1), rest[:, n, :, :]))
            for n in range(2):
                dve.wait(m_mid[n])
                done.append(dve.mark(dve.q.tensor_tensor(part(n, 2), rest[:, n, :, :], part(n, 1), ALU.subtract)))
                rest_free[n] = done[-1]
            for k, ms in enumerate((m_hi, m_mid, dict(enumerate(done)))):
                for n in range(2):
                    sp.wait(ms[n])
                    for dh in range(DH):
                        m = spill_parts[blk % 2].dma(sp.q.dma_start(
                            s["parts_d"][4 * blk:4 * blk + 4, 3 * n + k, dh].rearrange("c p t -> p c t"),
                            parts[:, blk % 2, 3 * n + k, dh, :].rearrange("p (c t) -> p c t", t=T)))
            stores[blk % 2] = (m,)
            if blk == 1:
                sp.wait(m_parts0, m_zeros)
                for c in range(2):
                    m_rows[c] = load_rows(p, s, c)
            m_parts0 = m

        for step, blk in ((norms, 0), (norms, 1), (project, 0), (project, 1), (norms, 2), (split, 0), (project, 2),
                          (norms, 3), (split, 1), (project, 3), (split, 2), (split, 3)):
            step(blk)
        sp.wait(spill[0].all(), spill[1].all(), spill_parts[0].all(), spill_parts[1].all(), al.all())
        return m_rows


def load_rows(p, s, c):
    q = s["rows_ld"][c % 2]
    src_all = s["parts_d"][c].rearrange("k h p t -> (k h) p t")
    for g in range(ROWG):
        src = src_all[:, RCH * g:RCH * (g + 1), :]
        for first, n in ((0, 12), (12, 4), (16, 2)):
            m = q.dma(p.sp.q.dma_start(s["rows"][32 * g + first:32 * g + first + n, c % 2, :, :], src[0:n]))
    return m


def selective_scan(p, a, s):
    pe, act, dve, pool, sp = p.pe, p.act, p.dve, p.pool, p.sp
    AT_A, AT_B, AT_C, LOAD_AT = LAG + 8, LAG + 9, LAG + 10, 1
    NB = 3
    with ExitStack() as ctx:
        sb = lambda name, shape, dt=F32: p.sb(name, shape, dt, ctx)
        h = sb("h", [P, 3, P // 2, W])
        decay = sb("decay", [P, NB, G, W])
        inp = sb("inp", [P, NB, G, W])
        w_out = sb("w_out", [P, DH, D])
        skip = sb("skip_c", [P, 2, DH, T])
        xres = sb("xres", [P, 2, D])
        y_sb = sb("y_sb", [P, 2, P])
        y_t = sb("y_t", [P, DH, T])
        x1o = sb("x1o", [P, Router.N, D])
        m_decay0 = pool.mark(pool.q.memset(decay[:, :, :, 0:1], 0.0))
        router = Router(p, a, ctx, s["gates"], s["slots"], s["ident"], s["eps"], s["disp_d"])
        z_used = [None]

        wo = p.count("wo0")
        wo.dma(act.q.dma_start(w_out[:, :, :], a["w_out"]))
        rows = s["rows"]
        skip_ld = [p.count(f"skipld{i}") for i in range(2)]
        xres_ld = [p.count(f"xresld{i}") for i in range(2)]
        x1_st = [p.count(f"x1st{i}") for i in range(Router.N)]
        x_flat = a["x"].rearrange("b s d -> (b s) d")

        bank_a = [p.banks[0], p.banks[1]]
        bank_x = [p.psum[:, 1024:2048], p.psum[:, 2048:3072]]
        bank_y, bank_z = p.banks[6], p.banks[7]
        exp_m, prod_m, inp_m, ready_m, scan_m, carry_m = {}, {}, {}, {}, {}, {}
        rows_m, skip_m, xres_m, pe_done = dict(s["m_rows"]), {}, {}, {}
        y_m, y_read, epi = {}, {}, {}
        store_m, resid_m, proj_m = {}, {}, {}

        def place_c(b):
            act.wait(y_m.get(CPB * b - 1))
            for dh in range(DH):
                r = slice(STATE * dh, STATE * (dh + 1))
                flat = s["cstat"][r, :, :].rearrange("p (q j) c -> p q (j c)", q=4)
                m = act.mark(act.q.copy(flat[:, :, dh:dh + 34 * 15 + 1:34],
                                        s["cmat"][r, b, :].rearrange("p (q j) -> p q j", q=4)))
            return m

        def half_slot(c, half):
            return c % 2 if half == 0 else 2

        def load_parts(c):
            sp.wait(pe_done[c - 2])
            rows_m[c] = load_rows(p, s, c)

        def load_epilogue(c):
            sp.wait(*(epi.get(c - 2, ())))
            skip_m[c] = skip_ld[c % 2].dma(sp.q.dma_start(skip[:, c % 2, :, :], s["skip_d"][:, :, c * T:(c + 1) * T]))
            xres_m[c] = xres_ld[c % 2].dma(sp.q.dma_start(xres[:, c % 2, :], x_flat[c * T:(c + 1) * T, :]))

        def stream(gi):
            c, k = divmod(gi, GROUPS)
            g = G * k // RCH
            pe.wait(rows_m[c])
            pe.wait(inp_m.get(gi - 2))
            for half in range(2):
                dp = G * k + 4 * half
                ins = pe.q.matmul(bank_x[gi % 2][:, 512 * half:512 * (half + 1)], s["sel"][:, g, :],
                                  rows[:, c % 2, dp % RCH:dp % RCH + 4, :], start=True, stop=True)
            bx = pe.mark(ins)
            for half in range(2):
                e = 2 * gi + half
                pe.wait(exp_m.get(e - 2))
                for j in range(4):
                    dp = G * k + 4 * half + j
                    ins = pe.q.matmul(bank_a[half][:, j * T:(j + 1) * T], s["astat"][:, dp, :],
                                      rows[:, c % 2, dp % RCH, :], start=True, stop=True)
                prod_m[e] = pe.mark(ins)
            if k == GROUPS - 1:
                pe_done[c] = prod_m[2 * gi + 1]
            pool.wait(scan_m.get(gi - NB))
            first = inp[:, gi % NB, :, 0:1]
            if c % CPB == 0:
                carry_m[gi] = pool.mark(pool.q.memset(first, 0.0))
            else:
                pool.wait(scan_m[gi - GROUPS])
                half, ch = divmod(G * k, P // 2)
                carry_m[gi] = pool.mark(pool.q.tensor_copy(
                    first, h[:, half_slot(c - 1, half), ch:ch + G, T:T + 1]))
            if gi >= LAG:
                scan(gi - LAG)
            bm = s["bmat"][:, c * T:(c + 1) * T].unsqueeze(1).broadcast_to([P, G, T])
            dst = inp[:, gi % NB, :, 1:W]
            src = bank_x[gi % 2].rearrange("p (j t) -> p j t", t=T)
            if k in ON_POOL:
                act.wait(bx, scan_m.get(gi - NB))
                inp_m[gi] = act.mark(act.q.copy(dst, src))
                pool.wait(inp_m[gi])
                ready_m[gi] = pool.mark(pool.q.tensor_tensor(dst, dst, bm, ALU.mult))
            else:
                dve.wait(bx, scan_m.get(gi - NB))
                inp_m[gi] = ready_m[gi] = dve.mark(dve.q.tensor_tensor(dst, src, bm, ALU.mult))
            for half in range(2):
                e = 2 * gi + half
                act.wait(prod_m[e], scan_m.get(gi - NB), m_decay0)
                exp_m[e] = act.mark(act.q.activation(
                    decay[:, gi % NB, 4 * half:4 * half + 4, 1:W],
                    bank_a[half][:, :].rearrange("p (j t) -> p j t", t=T), ACT.Exp))

        def scan(gi):
            c, k = divmod(gi, GROUPS)
            half, ch = divmod(G * k, P // 2)
            dve.wait(exp_m[2 * gi + 1], ready_m[gi], carry_m[gi], y_m.get(c - 2 if half == 0 else c - 1))
            flat = lambda v: v.rearrange("p g w -> p (g w)")
            scan_m[gi] = dve.mark(dve.q.tensor_tensor_scan(
                out=flat(h[:, half_slot(c, half), ch:ch + G, :]), data0=flat(decay[:, gi % NB, :, :]),
                data1=flat(inp[:, gi % NB, :, :]), initial=0.0, op0=ALU.mult, op1=ALU.add))

        def read_out(c, js):
            if js[0] == 0:
                pe.wait(scan_m[c * GROUPS + GROUPS - 1], y_read.get(c - 1))
                if c % CPB == 0:
                    pe.wait(place_c(c // CPB))
            slot = c % 2
            for j in js:
                for q in range(4):
                    tok = 16 * q + j
                    mov = h[:, slot:3:2 - slot, :, 1 + tok:1 + tok + 65:64].rearrange("p s d t -> p t s d")
                    ins = pe.q.matmul(bank_y[32 * q:32 * q + 32, 0:256].rearrange("p (t s d) -> p t s d", t=2, s=2),
                                      s["cstat"][:, tok, :], mov, start=j == 0, stop=j == 15)
            y_m[c] = pe.mark(ins) if js[-1] == 15 else None
            if y_m[c] is None:
                del y_m[c]

        def finish_a(c):
            act.wait(y_m[c], epi_t.get(c - 1))
            y_read[c] = act.mark(act.q.copy(y_sb[:, :, :].rearrange("p a b -> p (a b)"), bank_y[:, 0:256]))

        def finish_b(c):
            pe.wait(y_read[c], z_used[0])
            for th in range(2):
                ins = pe.q.transpose(bank_z[:, th * P:(th + 1) * P], y_sb[:, th, :], s["ident"][:, :])
            epi_t[c] = pe.mark(ins)
            act.wait(epi_t[c], proj_m.get(c - 1))
            for dh in range(DH):
                m = act.mark(act.q.copy(
                    y_t[:, dh, :].rearrange("p (th t) -> p th t", th=2),
                    bank_z[:, 0:256].rearrange("p (th t k) -> p th t k", th=2, k=2)[:, :, :, dh]))
            yt_m[c] = z_used[0] = m

        def finish_c(c):
            pe.wait(yt_m[c], skip_m[c], wo.all(), z_used[0])
            for dh in range(DH):
                pe.q.matmul(bank_z[:, 0:256], y_t[:, dh, :], w_out[:, dh, :], start=dh == 0, stop=False)
                ins = pe.q.matmul(bank_z[:, 0:256], skip[:, c % 2, dh, :], w_out[:, dh, :], start=False, stop=dh == 1)
            proj_m[c] = pe.mark(ins)
            n = Router.N
            dve.wait(proj_m[c], xres_m[c], store_m.get(c - n), *(router.normed.get(b) for b in range(len(router.BLOCKS))))
            resid_m[c] = z_used[0] = dve.mark(dve.q.tensor_tensor(x1o[:, c % n, :], bank_z[:, 0:256], xres[:, c % 2, :], ALU.add))
            epi[c] = (proj_m[c], resid_m[c])
            act.wait(resid_m[c])
            store_m[c] = x1_st[c % n].dma(act.q.dma_start(s["x1_d"][c * T:(c + 1) * T, :], x1o[:, c % n, :]))
            for b, (first, count) in enumerate(router.BLOCKS):
                if c == first + count - 1:
                    routing.append(router.steps(b, x1o, [resid_m[i] for i in range(first, c + 1)], bank_z, z_used))

        epi_t, yt_m, routing = {}, {}, []

        def advance():
            if routing and next(routing[0], "done") == "done":
                routing.pop(0)
        load_epilogue(0)
        load_epilogue(1)
        total = CHUNKS * GROUPS
        for gi in range(total + LAG):
            c, k = divmod(gi, GROUPS)
            if gi < total:
                stream(gi)
            else:
                scan(gi - LAG)
            for _ in range(1 if c < CHUNKS - 1 else 3):
                advance()
            if c >= 1 and gi < total:
                if LAG <= k < LAG + 8:
                    read_out(c - 1, range(2 * (k - LAG), 2 * (k - LAG) + 2))
                while k in (AT_B, AT_C) and z_used[0] == "written":
                    advance()
                if k == AT_A:
                    finish_a(c - 1)
                if k == AT_B:
                    finish_b(c - 1)
                if k == AT_C:
                    finish_c(c - 1)
            if k == LOAD_AT and 1 <= c < CHUNKS - 1:
                load_parts(c + 1)
            if k == AT_C and 1 <= c < CHUNKS - 1:
                load_epilogue(c + 1)
            if gi == total - 1:
                sp.wait(prod_m[2 * gi + 1])
                for e in range(2):
                    for w, name in zip(s["w12"], ("w1", "w2")):
                        s["w_ld"][e].dma(sp.q.dma_start(w[:, e], a[name][e]))
        c = CHUNKS - 1
        for j in range(16):
            read_out(c, [j])
            for _ in range(3):
                advance()
        while z_used[0] == "written":
            advance()
        finish_a(c)
        finish_b(c)
        finish_c(c)
        while routing:
            advance()
        act.wait(*(q.all() for q in x1_st))
        pool.wait(router.scattered.all())


def rest(p, a, out, s):
    nc, act = p.nc, p.act
    with ExitStack() as keep:
        sb = lambda name, shape, dt=F32: p.sb(name, shape, dt, keep)
        x1 = sb("x1", [P, TILES, D])
        wts = dict(wq=sb("wq", [P, DH, D]), wkv=sb("wkv", [P, DH, 2 * D]), wo=sb("wo", [P, DH, D]),
                   brow=sb("brow", [P, 3, D]),
                   c_decay_row=sb("dec_row", [P, SEQ]), c_decay_col=sb("dec_col", [P, CPB]), c_mask=sb("mask", [P, P]),
                   w_gu=sb("wgu", [P, 2, DH, FF]), w_down=sb("wd", [P, FT, D]))
        with ExitStack() as ctx:
            x1_ld, w_ld = p.count("x1ld"), p.count("w_rest")

            def later():
                x1_ld.dma(p.sp.q.dma_start(x1[:, :, :], s["x1_d"].rearrange("(i p) d -> p i d", p=P)))
                for name, tile in wts.items():
                    w_ld.dma(p.sp.q.dma_start(tile[tuple(slice(None) for _ in tile.shape)], a[name]))

            experts(p, a, s, ctx, later)
            m_x1, m_w = x1_ld.all(), w_ld.all()
            nc.all_engine_barrier()
        with ExitStack() as ctx:
            second_layer(p, s, ctx, x1, m_x1, wts, m_w, out)


class Router:
    N = 4
    BLOCKS = ((0, 4), (4, 4), (8, 4), (12, 3), (15, 1))

    def __init__(self, p, a, ctx, gates, slots, ident, eps, disp_d):
        self.p, self.gates, self.slots, self.ident, self.eps, self.disp_d = p, gates, slots, ident, eps, disp_d
        sb = lambda name, shape, dt=F32: p.sb("r_" + name, shape, dt, ctx)
        e3 = [P, self.N, EXPERTS]
        self.xl = sb("xl", [P, self.N, D])
        self.xt = sb("xt", [P, DH, P])
        self.wg = sb("wg", [P, DH, EXPERTS])
        self.tri_f, self.tri = sb("tri_f", [P, 2, P]), sb("tri", [P, 2, P], BF16)
        self.erow = sb("erow", [P, 2, EXPERTS])
        self.stats, self.mom = sb("stats", [P, self.N, 6]), sb("mom", [P, self.N, 2])
        self.sd, self.rstd = sb("sd", [P, self.N]), sb("rstd", [P, self.N])
        (self.logit, self.prob, self.oh0, self.oh1, self.place, self.kept, self.tmp, self.cum, self.cs,
         self.top) = (sb(n, e3) for n in ("logit", "prob", "oh0", "oh1", "place", "kept", "tmp", "cum", "cs", "top"))
        self.ind = sb("ind", e3, BF16)
        self.top_i = sb("top_i", e3, U32)
        self.top_f = sb("top_f", [P, self.N, 2])
        self.red = sb("red", [P, 3, self.N])
        self.ones = sb("ones", [P, self.N])
        self.before = sb("before", [P, EXPERTS])
        w = p.count("w_route")
        w.dma(p.act.q.dma_start(self.wg[:, :, :], a["w_gate8"]))
        w.dma(p.act.q.dma_start(self.tri_f[:, :, :], a["c_tri"]))
        self.m_w = w.dma(p.act.q.dma_start(self.erow[:, :, :], a["c_erow"]))
        p.pool.q.memset(self.ones[:, :], 1.0)
        p.pool.q.memset(self.before[:, :], 0.0)
        p.pool.wait(self.m_w)
        self.m_const = p.pool.mark(p.pool.q.tensor_copy(self.tri[:, :, :], self.tri_f[:, :, :]))
        self.scattered = p.count("scatter")
        self.normed = {}

    def steps(self, blk, x1, x1_ready, bank, used):
        first, n = self.BLOCKS[blk]
        p, n3 = self.p, n * EXPERTS
        pe, act, dve, pool = p.pe, p.act, p.dve, p.pool
        flat = lambda t: t.rearrange("p i e -> p (i e)")
        e3 = [P, n, EXPERTS]
        logit, prob, place, kept, tmp, cum, cs, top = (t[:, 0:n, :] for t in (
            self.logit, self.prob, self.place, self.kept, self.tmp, self.cum, self.cs, self.top))
        hots = (self.oh0[:, 0:n, :], self.oh1[:, 0:n, :])
        red, ind = self.red[:, :, 0:n], self.ind[:, 0:n, :]
        per_tile = lambda t: t.unsqueeze(2).broadcast_to(e3)
        per_expert = lambda t: t.unsqueeze(1).broadcast_to(e3)
        tiles = slice(first, first + n)
        at = first % self.N

        dve.wait(*x1_ready)
        for i in range(n):
            m = dve.mark(dve.q.bn_stats(self.stats[:, i, :], x1[:, at + i, :]))
        yield
        dve.wait(m)
        for i in range(n):
            m = dve.mark(dve.q.bn_aggr(self.mom[:, i, :], self.stats[:, i, :]))
        yield
        act.wait(m)
        m = act.mark(act.q.activation(self.sd[:, 0:n], self.mom[:, 0:n, 1], ACT.Sqrt, bias=self.eps[:, 0:1]))
        yield
        yield
        dve.wait(m)
        m = dve.mark(dve.q.reciprocal(self.rstd[:, 0:n], self.sd[:, 0:n]))
        yield
        dve.wait(m, self.scattered.all() if blk and at == 0 else None)
        for i in range(n):
            m = dve.mark(dve.q.tensor_scalar(self.xl[:, at + i, :], x1[:, at + i, :], self.mom[:, i, 0:1],
                                             self.rstd[:, i:i + 1], ALU.subtract, ALU.mult))
        self.normed[blk] = m_norm = m
        yield
        for i in range(n):
            pe.wait(m_norm, self.m_w, used[0])
            for dh in range(DH):
                ins = pe.q.transpose(bank[:, dh * P:(dh + 1) * P], self.xl[:, at + i, dh * P:(dh + 1) * P], self.ident[:, :])
            m = pe.mark(ins)
            used[0] = "written"
            yield
            act.wait(m)
            m = used[0] = act.mark(act.q.copy(self.xt[:, :, :].rearrange("p h t -> p (h t)"), bank[:, 0:2 * P]))
            yield
            pe.wait(m, used[0])
            for dh in range(DH):
                ins = pe.q.matmul(bank[:, 256:256 + EXPERTS], self.xt[:, dh, :], self.wg[:, dh, :],
                                  start=dh == 0, stop=dh == 1)
            m = pe.mark(ins)
            used[0] = "written"
            yield
            dve.wait(m)
            m = used[0] = dve.mark(dve.q.tensor_copy(logit[:, i, :], bank[:, 256:256 + EXPERTS]))

        def v(ins):
            return dve.mark(ins)

        yield
        dve.wait(m, self.m_const)
        m = v(dve.q.tensor_reduce(red[:, 0, :], logit[:, :, :], AX.X, ALU.max))
        yield
        dve.wait(m)
        m = v(dve.q.tensor_tensor(logit[:, :, :], logit[:, :, :], per_tile(red[:, 0, :]), ALU.subtract))
        yield
        act.wait(m)
        m = act.mark(act.q.activation(prob[:, :, :], logit[:, :, :], ACT.Exp))
        yield
        dve.wait(m)
        m = v(dve.q.tensor_reduce(red[:, 1, :], prob[:, :, :], AX.X, ALU.add))
        yield
        dve.wait(m)
        m = v(dve.q.reciprocal(red[:, 2, :], red[:, 1, :]))
        yield
        dve.wait(m)
        m = v(dve.q.tensor_tensor(prob[:, :, :], prob[:, :, :], per_tile(red[:, 2, :]), ALU.mult))
        yield
        dve.wait(m)
        for i in range(n):
            m = v(dve.q.max(top[:, i, :], prob[:, i, :]))
        yield
        dve.wait(m)
        for i in range(n):
            m = v(dve.q.max_index(self.top_i[:, i, :], top[:, i, :], prob[:, i, :]))
        yield
        dve.wait(m)
        m = v(dve.q.tensor_copy(self.top_f[:, 0:n, :], self.top_i[:, 0:n, 0:2]))
        yield
        dve.wait(m)
        number, base = per_expert(self.erow[:, 0, :]), per_expert(self.erow[:, 1, :])
        for k in range(2):
            m = v(dve.q.tensor_tensor(hots[k], number, per_tile(self.top_f[:, 0:n, k]), ALU.is_equal))
        yield
        dve.wait(m)
        m = v(dve.q.tensor_tensor(ind[:, :, :], hots[0], hots[1], ALU.add))
        yield
        pe.wait(m, self.m_const, used[0])
        pe.q.matmul(bank[:, 256:256 + n3], self.tri[:, 0, :], flat(ind), start=True, stop=True)
        m = pe.mark(pe.q.matmul(bank[:, 320:320 + n3], self.tri[:, 1, :], flat(ind), start=True, stop=True))
        used[0] = "written"
        yield
        dve.wait(m)
        v(dve.q.tensor_copy(flat(cs), bank[:, 320:320 + n3]))
        m = used[0] = v(dve.q.tensor_copy(flat(place), bank[:, 256:256 + n3]))
        yield
        dve.wait(m)
        for e in range(EXPERTS):
            m = v(dve.q.tensor_tensor_scan(out=cum[:, :, e], data0=self.ones[:, 0:n], data1=cs[:, :, e],
                                           initial=self.before[:, e:e + 1], op0=ALU.mult, op1=ALU.add))
        yield
        dve.wait(m)
        m2 = v(dve.q.tensor_copy(self.before[:, :], cum[:, n - 1, :]))
        m = v(dve.q.tensor_tensor(tmp[:, :, :], cum[:, :, :], cs[:, :, :], ALU.subtract))
        yield
        dve.wait(m)
        m = v(dve.q.tensor_tensor(place[:, :, :], place[:, :, :], tmp[:, :, :], ALU.add))
        yield
        dve.wait(m)
        m = v(dve.q.tensor_scalar(kept[:, :, :], place[:, :, :], float(CAP), None, ALU.is_lt))
        yield
        dve.wait(m)
        m = v(dve.q.tensor_tensor(place[:, :, :], place[:, :, :], base, ALU.add))
        yield
        for k in range(2):
            dve.wait(m)
            m = v(dve.q.tensor_tensor(tmp[:, :, :], hots[k], place[:, :, :], ALU.mult))
            yield
            dve.wait(m)
            m = v(dve.q.tensor_reduce(red[:, 0, :], tmp[:, :, :], AX.X, ALU.add))
            yield
            dve.wait(m)
            m = v(dve.q.tensor_tensor(tmp[:, :, :], hots[k], kept[:, :, :], ALU.mult))
            yield
            dve.wait(m)
            m = v(dve.q.tensor_reduce(red[:, 1, :], tmp[:, :, :], AX.X, ALU.add))
            yield
            dve.wait(m)
            v(dve.q.tensor_tensor(self.gates[:, k, tiles], top[:, :, k], red[:, 1, :], ALU.mult))
            m = v(dve.q.scalar_tensor_tensor(red[:, 2, :], red[:, 0, :], float(-SLOTS), red[:, 1, :], ALU.add,
                                             ALU.mult))
            yield
            dve.wait(m)
            m = v(dve.q.tensor_scalar(self.slots[:, k, tiles], red[:, 2, :], float(SLOTS), None, ALU.add))
            yield
        pool.wait(m)
        for i in range(n):
            for k in range(2):
                t = first + i
                self.scattered.dma(pool.q.indirect_dma_start(
                    out=self.disp_d, out_offset=bass.IndirectOffsetOnAxis(ap=self.slots[:, k, t:t + 1], axis=0),
                    in_=self.xl[:, at + i, :], in_offset=None, bounds_check=SLOTS - 1, oob_is_err=False))
                yield


def experts(p, a, s, ctx, later):
    pe, act, dve, pool, sp = p.pe, p.act, p.dve, p.pool, p.sp
    sb = lambda name, shape, dt=F32: p.sb(name, shape, dt, ctx)
    NW = 2
    w1, w2 = expert_weights(s["shared"])
    xd = sb("xd", [P, 2, ST, D])
    xdt = sb("xdt", [P, 2, DH, CAP])
    hid = sb("hid", [P, 2, FT, CAP])
    eo = sb("eo", [P, 2, ST, D])
    ring = p.ring(8)
    w1_ld, w2_ld, xd_ld, eo_st = ([p.count(f"{n}{i}") for i in range(2)] for n in ("w1", "w2", "xd", "eo"))
    half_cap = CAP // 2
    m_w1, m_w2 = ({e: s["w_ld"][e].all() for e in range(NW)} for _ in range(2))
    m_xd, m_xt, m_up, m_down, m_tr, m_store = {}, {}, {}, {}, {}, {}
    hid_m, turn = {}, [0]

    def evacuate(dst, src, b, wait, relu=False):
        turn[0] += 1
        if turn[0] % 2:
            act.wait(*wait)
            m = act.mark(act.q.activation(dst, src, ACT.Relu) if relu else act.q.copy(dst, src))
        else:
            dve.wait(*wait)
            m = dve.mark(dve.q.tensor_scalar(dst, src, 0.0, None, ALU.max) if relu else dve.q.tensor_copy(dst, src))
        ring.read_by(b, m)
        return m

    def load(e):
        if e >= EXPERTS:
            return
        sp.wait(m_tr.get(e - 2))
        m_xd[e] = xd_ld[e % 2].dma(sp.q.dma_start(
            xd[:, e % 2, :, :], s["disp_d"][e * CAP:(e + 1) * CAP, :].rearrange("(s p) d -> p s d", p=P)))
        if e < NW:
            return
        sp.wait(m_up[e - NW])
        m_w1[e] = w1_ld[e % 2].dma(sp.q.dma_start(w1[:, e % NW, :, :], a["w1"][e]))
        sp.wait(m_down[e - NW])
        m_w2[e] = w2_ld[e % 2].dma(sp.q.dma_start(w2[:, e % NW, :, :], a["w2"][e]))

    def transposes(e):
        if e >= EXPERTS:
            return
        pe.wait(m_xd[e])
        ms = []
        for dh in range(DH):
            for first, n in ((0, 4), (4, 1)):
                b, bank = ring.take()
                for j in range(n):
                    ins = pe.q.transpose(bank[:, j * P:(j + 1) * P], xd[:, e % 2, first + j, dh * P:(dh + 1) * P],
                                         s["ident"][:, :])
                m = pe.mark(ins)
                ms.append(evacuate(xdt[:, e % 2, dh, first * P:(first + n) * P], bank[:, 0:n * P], b,
                                   (m, m_up.get(e - 2))))
        m_tr[e] = m
        m_xt[e] = ms

    def up(e):
        pe.wait(m_w1[e], *m_xt[e])
        hid_m[e] = []
        for f in range(FT):
            for c in range(2):
                b, bank = ring.take()
                cs = slice(c * half_cap, (c + 1) * half_cap)
                for dh in range(DH):
                    ins = pe.q.matmul(bank[:, 0:half_cap], w1[:, e % NW, dh, f * P:(f + 1) * P],
                                      xdt[:, e % 2, dh, cs], start=dh == 0, stop=dh == 1)
                m = pe.mark(ins)
                hid_m[e].append(evacuate(hid[:, e % 2, f, cs], bank[:, 0:half_cap], b, (m, m_down.get(e - 2)), True))
        m_up[e] = m

    def down(e):
        pe.wait(m_w2[e], *hid_m[e])
        ms = []
        for st in range(ST):
            b, bank = ring.take()
            for f in range(FT):
                ins = pe.q.matmul(bank[:, 0:D], hid[:, e % 2, f, st * P:(st + 1) * P], w2[:, e % NW, f, :],
                                  start=f == 0, stop=f == FT - 1)
            m = pe.mark(ins)
            ms.append(evacuate(eo[:, e % 2, st, :], bank[:, 0:D], b, (m, m_store.get(e - 2))))
        m_down[e] = m
        sp.wait(*ms)
        m_store[e] = eo_st[e % 2].dma(sp.q.dma_start(
            s["eout_d"][e * CAP:(e + 1) * CAP, :].rearrange("(s p) d -> p s d", p=P), eo[:, e % 2, :, :]))

    load(0)
    load(1)
    later()
    transposes(0)
    for e in range(EXPERTS):
        up(e)
        transposes(e + 1)
        down(e)
        load(e + 2)
    sp.wait(eo_st[0].all(), eo_st[1].all())


def second_layer(p, s, ctx, x1, m_x1, wts, m_w, out):
    pe, act, dve, pool, sp = p.pe, p.act, p.dve, p.pool, p.sp
    sb = lambda name, shape, dt=F32: p.sb(name, shape, dt, ctx)
    NT = 4
    BLOCKS = TILES // NT
    gates, slots, ident = s["gates"], s["slots"], s["ident"]
    wq, wkv, wo, brow, dec_row, dec_col, mask, wgu, wd = wts.values()
    xb = sb("xb", [P, TILES, D])
    got = sb("got", [P, 2, 2, NT, D])
    xl = sb("xl", [P, 2, NT, D])
    xt = sb("xt", [P, 2, DH, 512])
    qt = sb("qt", [P, 2, TOK])
    kv = sb("kv", [P, 2, 2, D])
    va = sb("va", [P, 2, 2, P + 1])
    bd = sb("bd", [P, 2, P])
    kden = sb("kden", [P, 2, P])
    den = sb("den", [P, 2, 512])
    at = sb("at", [P, 2, 2, 512])
    sil = sb("sil", [P, 2, 512])
    gt = s["shared"].rearrange("p (b f t) -> p b f t", b=2, f=FT)
    o = sb("o", [P, 2, NT, D])
    norms = [dict(stats=sb(f"stats{n}", [P, TILES, 6]), mom=sb(f"mom{n}", [P, TILES, 2]), sd=sb(f"sd{n}", [P, TILES]),
                  rstd=sb(f"rstd{n}", [P, TILES]), eps=s["eps"]) for n in range(2)]
    ring = p.ring(6)
    bank_kv = p.banks[6:8]
    m_ones = pool.mark(pool.q.memset(va[:, :, :, P:P + 1], 1.0))
    for e in (pe, act, dve, pool):
        e.wait(m_w)
    dve.wait(m_x1, m_ones)
    act.q.activation(sb("warm", [P, 1])[:, :], s["eps"][:, 0:1], ACT.Sqrt)
    rows = {}
    tiles_of = lambda blk: list(range(NT * blk, NT * (blk + 1)))
    got_free, x2_m, x2b_m, x3_m = {}, {}, {}, {}
    xl_free, xt_free, xl_use, xl_m, xt_m = {}, {}, [0], {}, {}
    q_m, kv_free, at_m, at_free, gt_m, gt_free, sil_free, down_m = {}, {}, {}, {}, {}, {}, {}, {}
    bd_m, kv_read = {}, []
    out_v = out.rearrange("b (i p) d -> p (b i) d", p=P)
    st = [p.count(f"out{i}") for i in range(2)]

    def gather(blk):
        pool.wait(*got_free.get(blk - 2, ()))
        for n, i in enumerate(tiles_of(blk)):
            c = p.count(f"gather{i}")
            for k in range(2):
                rows[i] = c.dma(pool.q.indirect_dma_start(
                    out=got[:, blk % 2, k, n, :], out_offset=None, in_=s["eout_d"],
                    in_offset=bass.IndirectOffsetOnAxis(ap=slots[:, k, i:i + 1], axis=0)))

    def combine(blk):
        for n, i in enumerate(tiles_of(blk)):
            dve.wait(rows[i])
            first = dve.mark(dve.q.scalar_tensor_tensor(xb[:, i, :], got[:, blk % 2, 0, n, :], gates[:, 0, i:i + 1],
                                                           x1[:, i, :], ALU.mult, ALU.add))
            dve.wait(first)
            x2_m[i] = dve.mark(dve.q.scalar_tensor_tensor(xb[:, i, :], got[:, blk % 2, 1, n, :], gates[:, 1, i:i + 1],
                                                          xb[:, i, :], ALU.mult, ALU.add))
        got_free[blk] = (x2_m[i],)

    def add_bias(blk):
        for i in tiles_of(blk):
            pool.wait(x2_m[i])
            x2b_m[i] = pool.mark(pool.q.tensor_tensor(x1[:, i, :], xb[:, i, :], brow[:, 2, :], ALU.add))

    def norm(key, blk, which, ready):
        tiles = tiles_of(blk)
        layer_norm_stats(p, xb, tiles, src_ready=ready, **norms[which])
        u = xl_use[0] % 2
        xl_use[0] += 1
        dve.wait(xl_free.get(u))
        for n, i in enumerate(tiles):
            m = dve.mark(dve.q.tensor_scalar(xl[:, u, n, :], xb[:, i, :], norms[which]["mom"][:, i, 0:1],
                                             norms[which]["rstd"][:, i:i + 1], ALU.subtract, ALU.mult))
        xl_m[key] = (u, m)

    def transposes(key):
        u, m = xl_m[key]
        pe.wait(m)
        ms = []
        for dh in range(DH):
            bk, bank = ring.take()
            for n in range(NT):
                ins = pe.q.transpose(bank[:, n * P:(n + 1) * P], xl[:, u, n, dh * P:(dh + 1) * P], ident[:, :])
            m = pe.mark(ins)
            act.wait(m, xt_free.get(u))
            ms.append(act.mark(act.q.copy(xt[:, u, dh, :], bank[:, :])))
            ring.read_by(bk, ms[-1])
        xl_free[u] = m
        xt_m[key] = (u, ms)

    def project_qkv(blk):
        u, ms = xt_m["a", blk]
        pe.wait(*ms)
        t5 = slice(512 * blk, 512 * (blk + 1))
        for hh in range(2):
            bk, bank = ring.take()
            for dh in range(DH):
                ins = pe.q.matmul(bank[:, :], wq[:, dh, hh * P:(hh + 1) * P], xt[:, u, dh, :],
                                  start=dh == 0, stop=dh == 1)
            m = pe.mark(ins)
            act.wait(m)
            m = act.mark(act.q.activation(qt[:, hh, t5], bank[:, :], ACT.Relu, bias=s["bq"][:, hh:hh + 1]))
            ring.read_by(bk, m)
            dve.wait(m)
            pos = 512 * blk % SEQ
            q_m[blk, hh] = dve.mark(dve.q.tensor_tensor(qt[:, hh, t5], qt[:, hh, t5], dec_row[:, pos:pos + 512],
                                                          ALU.mult))
        kv_m = {}
        for n, i in enumerate(tiles_of(blk) + [None]):
            if i is not None:
                bk, bank = ring.take()
                for dh in range(DH):
                    ins = pe.q.matmul(bank[:, :], xt[:, u, dh, n * P:(n + 1) * P], wkv[:, dh, :],
                                      start=dh == 0, stop=dh == 1)
                m = pe.mark(ins)
                w = i % 2
                dve.wait(m, kv_free.get(w))
                m1 = dve.mark(dve.q.tensor_tensor(kv[:, w, 0, :], bank[:, 0:D], brow[:, 0, :], ALU.add))
                m2 = dve.mark(dve.q.tensor_tensor(
                    va[:, w, :, 0:P], bank[:, D:2 * D].rearrange("p (h e) -> p h e", h=2),
                    brow[:, 1, :].rearrange("p (h e) -> p h e", h=2), ALU.add))
                ring.read_by(bk, m2)
                dve.wait(m1)
                kv_m[i] = dve.mark(dve.q.tensor_scalar(kv[:, w, 1, :], kv[:, w, 0, :], 0.0,
                                                       dec_col[:, i % CPB:i % CPB + 1], ALU.max, ALU.mult))
                xt_free[u] = m
            if n:
                j = NT * blk + n - 1
                w = j % 2
                pe.wait(kv_m[j], *kv_read)
                for hh in range(2):
                    ins = pe.q.matmul(bank_kv[hh][:, 0:P + 1], kv[:, w, 1, hh * P:(hh + 1) * P], va[:, w, hh, :],
                                      start=j % CPB == 0, stop=j % CPB == CPB - 1)
                kv_free[w] = pe.mark(ins)

    def heads(b):
        dve.wait(kv_free[1], bd_m.get("used"))
        for hh in range(2):
            dve.mark(dve.q.tensor_tensor(bd[:, hh, :], bank_kv[hh][:, 0:P], mask[:, :], ALU.mult))
            m = dve.mark(dve.q.tensor_scalar(kden[:, hh, :], mask[:, :], bank_kv[hh][:, P:P + 1], None, ALU.mult))
        bd_m["m"] = m
        kv_read[:] = [m]

    def attend(blk):
        t5 = slice(512 * blk, 512 * (blk + 1))
        pe.wait(bd_m["m"])
        at_m[blk] = []
        for hh in range(2):
            pe.wait(q_m[blk, hh])
            bk1, bank1 = ring.take()
            m1 = pe.mark(pe.q.matmul(bank1[:, :], kden[:, hh, :], qt[:, hh, t5], start=True, stop=True))
            bk2, bank2 = ring.take()
            m2 = bd_m["used"] = pe.mark(pe.q.matmul(bank2[:, :], bd[:, hh, :], qt[:, hh, t5], start=True, stop=True))
            dve.wait(m1)
            m = dve.mark(dve.q.tensor_scalar(den[:, hh, :], bank1[:, :], 1e-6, None, ALU.add))
            ring.read_by(bk1, m)
            dve.wait(m)
            m = dve.mark(dve.q.reciprocal(den[:, hh, :], den[:, hh, :]))
            dve.wait(m, m2, at_free.get(blk % 2))
            m = dve.mark(dve.q.tensor_tensor(at[:, blk % 2, hh, :], bank2[:, :], den[:, hh, :], ALU.mult))
            ring.read_by(bk2, m)
            at_m[blk].append(m)

    def attention_out(blk):
        pe.wait(*at_m[blk])
        for n, i in enumerate(tiles_of(blk)):
            bk, bank = ring.take()
            for hh in range(2):
                ins = pe.q.matmul(bank[:, 0:D], at[:, blk % 2, hh, n * P:(n + 1) * P], wo[:, hh, :],
                                  start=hh == 0, stop=hh == 1)
            m = at_free[blk % 2] = pe.mark(ins)
            dve.wait(m, x2b_m[i])
            x3_m[i] = dve.mark(dve.q.tensor_tensor(xb[:, i, :], bank[:, 0:D], x1[:, i, :], ALU.add))
            ring.read_by(bk, x3_m[i])

    def gate_up(blk):
        u, ms = xt_m["m", blk]
        pe.wait(*ms)
        gt_m[blk] = []
        for f in range(FT):
            pair = []
            for j in range(2):
                bk, bank = ring.take()
                for dh in range(DH):
                    ins = pe.q.matmul(bank[:, :], wgu[:, j, dh, f * P:(f + 1) * P], xt[:, u, dh, :],
                                      start=dh == 0, stop=dh == 1)
                pair.append((bk, bank, pe.mark(ins)))
            w = f % 2
            act.wait(pair[0][2], sil_free.get(w))
            m = act.mark(act.q.activation(sil[:, w, :], pair[0][1][:, :], ACT.Silu))
            ring.read_by(pair[0][0], m)
            dve.wait(m, pair[1][2], gt_free.get(blk % 2))
            m = dve.mark(dve.q.tensor_tensor(gt[:, blk % 2, f, :], pair[1][1][:, :], sil[:, w, :], ALU.mult))
            ring.read_by(pair[1][0], m)
            sil_free[w] = m
            gt_m[blk].append(m)
        xt_free[u] = pair[1][2]

    def down(blk):
        pe.wait(*gt_m[blk])
        for n, i in enumerate(tiles_of(blk)):
            bk, bank = ring.take()
            for f in range(FT):
                ins = pe.q.matmul(bank[:, 0:D], gt[:, blk % 2, f, n * P:(n + 1) * P], wd[:, f, :],
                                  start=f == 0, stop=f == FT - 1)
            m = pe.mark(ins)
            dve.wait(m, down_m.get(blk - 2))
            mo = dve.mark(dve.q.tensor_tensor(o[:, blk % 2, n, :], bank[:, 0:D], xb[:, i, :], ALU.add))
            ring.read_by(bk, mo)
            if n % 2:
                sp.wait(mo)
                stored = st[blk % 2].dma(sp.q.dma_start(out_v[:, i - 1:i + 1, :], o[:, blk % 2, n - 1:n + 1, :]))
        gt_free[blk % 2] = m
        down_m[blk] = stored

    def ready(blk):
        combine(blk)
        norm(("a", blk), blk, 0, x2_m)

    gather(0)
    gather(1)
    ready(0)
    transposes(("a", 0))
    ready(1)
    gather(2)
    gather(3)
    project_qkv(0)
    transposes(("a", 1))
    ready(2)
    project_qkv(1)
    add_bias(0)
    add_bias(1)
    heads(0)
    transposes(("a", 2))
    attend(0)
    project_qkv(2)
    ready(3)
    attend(1)
    attention_out(0)
    transposes(("a", 3))
    attention_out(1)
    norm(("m", 0), 0, 1, x3_m)
    project_qkv(3)
    add_bias(2)
    add_bias(3)
    heads(1)
    transposes(("m", 0))
    attend(2)
    attend(3)
    gate_up(0)
    norm(("m", 1), 1, 1, x3_m)
    attention_out(2)
    attention_out(3)
    for blk in range(BLOCKS):
        if blk:
            gate_up(blk)
        if blk + 1 < BLOCKS:
            transposes(("m", blk + 1))
        if blk + 2 < BLOCKS:
            norm(("m", blk + 2), blk + 2, 1, x3_m)
        down(blk)
    sp.wait(st[0].all(), st[1].all())


def lay_out(v):
    f = np.ascontiguousarray
    halves_t = lambda w: w.T.reshape(DH, P, w.shape[0]).transpose(1, 0, 2)
    col = lambda w: w.reshape(DH, P).T
    xp = v["L0_attn_x_proj_w"]
    dt_w, b_w, c_w = xp[:RANK], xp[RANK:RANK + STATE], xp[RANK + STATE:]
    proj = np.concatenate([dt_w, b_w, b_w, c_w, c_w])
    sel = np.zeros((P, ROWG, P), np.float32)
    for g in range(ROWG):
        for r in range(6, 12):
            sel[32 * g + r, g, STATE * (r % 2):STATE * (r % 2) + STATE] = 1
    z = {
        "x": v["L0_attn_x"],
        "c_ident": np.eye(P, dtype=np.float32),
        "c_sel": sel,
        "cols": np.stack([col(v[n]) for n in ("L0_attn_norm_w", "L0_attn_norm_b", "L0_attn_D_param",
                                              "L0_attn_dt_proj_b", "L1_attn_bq")], 1),
        "w_proj": halves_t(proj).reshape(P, DH, 3, P),
        "w_dt": v["L0_attn_dt_proj_w"].T,
        "a_log": v["L0_attn_A_log"].reshape(DH, P, STATE).transpose(1, 0, 2),
        "w_out": halves_t(v["L0_attn_out_proj_w"]),
    }
    pos = np.arange(SEQ, dtype=np.float32)
    decay = np.exp(-pos / np.float32(SEQ)).astype(np.float32)
    head = np.arange(P) // DK
    bk, bv, bo = (v["L1_attn_" + n] for n in ("bk", "bv", "bo"))
    z |= {
        "c_tri": np.stack([np.triu(np.ones((P, P)), 1), np.ones((P, P))], 1).astype(np.float32),
        "c_erow": np.broadcast_to(np.stack([np.arange(EXPERTS), CAP * np.arange(EXPERTS)]).astype(np.float32),
                                  (P, 2, EXPERTS)),
        "c_decay_row": np.broadcast_to(decay, (P, SEQ)),
        "c_decay_col": decay.reshape(CPB, P).T,
        "c_mask": (head[:, None] == head[None, :]).astype(np.float32),
        "w_gate8": v["L0_ffn_Wg"].reshape(DH, P, EXPERTS).transpose(1, 0, 2),
        "w1": v["L0_ffn_w1"].reshape(EXPERTS, DH, P, FF).transpose(0, 2, 1, 3),
        "w2": v["L0_ffn_w2"].reshape(EXPERTS, FT, P, D).transpose(0, 2, 1, 3),
        "wq": halves_t(v["L1_attn_Wq"]),
        "wkv": halves_t(np.concatenate([v["L1_attn_Wk"], v["L1_attn_Wv"]])),
        "wo": halves_t(v["L1_attn_Wo"]),
        "brow": np.broadcast_to(np.stack([bk, bv, bo]), (P, 3, D)),
        "w_gu": np.stack([halves_t(v["L1_ffn_w_gate"]), halves_t(v["L1_ffn_w_up"])], 1),
        "w_down": v["L1_ffn_w_down"].T.reshape(FT, P, D).transpose(1, 0, 2),
    }
    return {k: f(x) for k, x in z.items()}


def kernel(**inputs):
    import concourse.bacc as bacc
    from concourse.bass_utils import run_bass_kernel_spmd
    arrays = lay_out({k: np.asarray(v) for k, v in inputs.items()})
    nc = bacc.Bacc("TRN2", target_bir_lowering=False, num_devices=1)
    aps = {k: nc.dram_tensor("in_" + k, x.shape, mybir.dt.from_np(x.dtype), kind="ExternalInput").ap()
           for k, x in arrays.items()}
    out = nc.dram_tensor("out", [BATCH, SEQ, D], F32, kind="ExternalOutput").ap()
    build(nc, aps, out)
    r = run_bass_kernel_spmd(nc, [{"in_" + k: x for k, x in arrays.items()}], core_ids=[0])
    return r.results[0]["out"]
```
